# Optimizing a Trainium2 kernel written in Bass

```python
import numpy as np
import jax
import jax.numpy as jnp

def _softmax(x, axis=-1):
    return jax.nn.softmax(x, axis=axis)

def _gelu(x):
    return jax.nn.gelu(x, approximate=True)

def _silu(x):
    return jax.nn.silu(x)

def _sigmoid(x):
    return jax.nn.sigmoid(x)

def _layernorm(x, axis=-1, eps=1e-05):
    m = jnp.mean(x, axis=axis, keepdims=True)
    v = jnp.var(x, axis=axis, keepdims=True)
    return (x - m) / jnp.sqrt(v + eps)

def _scatter_add(tgt, idx, src, axis=0):
    return tgt.at[idx].add(src)

def _segment_sum(src, seg, n):
    return jax.ops.segment_sum(src, seg, n)
kernel_name = 'mk_conv_preact_d2_conv_nchw64_r2_6d9216'

def setup_inputs(seed: int=0):
    np.random.seed(seed)
    _w = jnp.asarray

    def _rec_inputs():
        import jax
        import jax.numpy as jnp
        _gk = jax.random.key(seed)
        x = 7.22e-05 + 1 * jax.random.normal(jax.random.fold_in(_gk, 1), (8, 32, 64, 64), jnp.float32)
        return x
    x = _rec_inputs()

    def _L0_conv_setup():
        import jax, jax.numpy as jnp
        import numpy as np
        K = 3
        R = 4
        C_IN = 32
        C_OUT = 32
        B = 8
        H = 64
        W = 64
        MIN_HYP = 0.1
        TEMP = 1.0
        EPS = 0.0001

        def _forward(x, gate_w, gate_b, value_w, geom_w, geom_b, pw_w, pw_b):
            Bb, C, Hh, Ww = x.shape
            L = Hh * Ww
            S = K * K
            pad = K // 2
            gate = jnp.einsum('bchw,rc->brhw', x, gate_w) + gate_b[None, :, None, None]
            mu = jax.nn.softmax(gate / TEMP, axis=1).reshape(Bb, R, 1, L)
            v = jnp.einsum('bchw,dc->bdhw', x, value_w)
            vp = jnp.pad(v, ((0, 0), (0, 0), (pad, pad), (pad, pad)))
            patches = jnp.stack([vp[:, :, i:i + Hh, j:j + Ww] for i in range(K) for j in range(K)], axis=2).reshape(Bb, C, S, L)
            g = jnp.einsum('bchw,gc->bghw', x, geom_w) + geom_b[None, :, None, None]
            g = g.reshape(Bb, 3, R, L)
            theta, raw_base, raw_hyp = (g[:, 0], g[:, 1], g[:, 2])
            base = jax.nn.softplus(raw_base) + EPS
            hyper = jax.nn.softplus(raw_hyp) + MIN_HYP
            sig_u = (base * jnp.exp(hyper))[:, :, None, :]
            sig_s = (base * jnp.exp(-hyper))[:, :, None, :]
            ct = jnp.cos(theta)[:, :, None, :]
            st = jnp.sin(theta)[:, :, None, :]
            offs = np.array([(r - pad, c - pad) for r in range(K) for c in range(K)], dtype=np.float32)
            dy = jnp.asarray(offs[:, 0]).reshape(1, 1, S, 1)
            dx = jnp.asarray(offs[:, 1]).reshape(1, 1, S, 1)
            pu = ct * dx + st * dy
            ps = -st * dx + ct * dy
            kern = jnp.exp(-(pu / sig_u) ** 2 - (ps / sig_s) ** 2)
            w = mu * kern
            w = w / (jnp.sum(w, axis=(1, 2), keepdims=True) + 1e-06)
            agg = jnp.einsum('brsl,bcsl->brcl', w, patches).reshape(Bb, R * C, Hh, Ww)
            return jnp.einsum('bkhw,ok->bohw', agg, pw_w) + pw_b[None, :, None, None]
        key = jax.random.key(seed)
        ks = jax.random.split(key, 8)
        sc = 0.05
        return {'x': jax.random.normal(ks[0], (B, C_IN, H, W), jnp.float32), 'gate_w': jax.random.normal(ks[1], (R, C_IN), jnp.float32) * sc, 'gate_b': jax.random.normal(ks[2], (R,), jnp.float32) * sc, 'value_w': jax.random.normal(ks[3], (C_IN, C_IN), jnp.float32) * sc, 'geom_w': jax.random.normal(ks[4], (3 * R, C_IN), jnp.float32) * sc, 'geom_b': jax.random.normal(ks[5], (3 * R,), jnp.float32) * sc, 'pw_w': jax.random.normal(ks[6], (C_OUT, R * C_IN), jnp.float32) * sc, 'pw_b': jax.random.normal(ks[7], (C_OUT,), jnp.float32) * sc}
    _L0_conv_all = _L0_conv_setup()
    _L0_conv_in = {k: v for k, v in _L0_conv_all.items() if k in ('gate_w', 'gate_b', 'value_w', 'geom_w', 'geom_b', 'pw_w', 'pw_b')}
    del _L0_conv_all

    def _L1_conv_setup():
        import jax, jax.numpy as jnp
        import numpy as np
        DN = ('NCHW', 'OIHW', 'NCHW')

        def conv3x3(x, w):
            return jax.lax.conv_general_dilated(x, w, window_strides=(1, 1), padding=((1, 1), (1, 1)), dimension_numbers=DN)
        key = jax.random.key(seed)
        kx, k1, k2, k3 = jax.random.split(key, 4)
        N, Cin, Cmid, Cout, H, W = (16, 32, 64, 32, 112, 112)
        x = jax.random.normal(kx, (N, Cin, H, W), dtype=jnp.float32)
        w1 = jax.random.normal(k1, (Cmid, Cin, 3, 3), dtype=jnp.float32) / np.sqrt(Cin * 9)
        w2 = jax.random.normal(k2, (Cmid, Cmid, 3, 3), dtype=jnp.float32) / np.sqrt(Cmid * 9)
        w3 = jax.random.normal(k3, (Cout, Cmid, 3, 3), dtype=jnp.float32) / np.sqrt(Cmid * 9)
        return {'x': x, 'w1': w1, 'w2': w2, 'w3': w3}
    _L1_conv_all = _L1_conv_setup()
    _L1_conv_in = {k: v for k, v in _L1_conv_all.items() if k in ('w1', 'w2', 'w3')}
    del _L1_conv_all
    return {'x': x, 'L0_conv_gate_w': _L0_conv_in['gate_w'], 'L0_conv_gate_b': _L0_conv_in['gate_b'], 'L0_conv_value_w': _L0_conv_in['value_w'], 'L0_conv_geom_w': _L0_conv_in['geom_w'], 'L0_conv_geom_b': _L0_conv_in['geom_b'], 'L0_conv_pw_w': _L0_conv_in['pw_w'], 'L0_conv_pw_b': _L0_conv_in['pw_b'], 'L1_conv_w1': _L1_conv_in['w1'], 'L1_conv_w2': _L1_conv_in['w2'], 'L1_conv_w3': _L1_conv_in['w3']}

def reference(x, L0_conv_gate_w, L0_conv_gate_b, L0_conv_value_w, L0_conv_geom_w, L0_conv_geom_b, L0_conv_pw_w, L0_conv_pw_b, L1_conv_w1, L1_conv_w2, L1_conv_w3):
    import jax
    import jax.numpy as jnp

    def _L0_conv_ref(x, gate_w, gate_b, value_w, geom_w, geom_b, pw_w, pw_b):
        import jax, jax.numpy as jnp
        import numpy as np
        K = 3
        R = 4
        C_IN = 32
        C_OUT = 32
        B = 8
        H = 64
        W = 64
        MIN_HYP = 0.1
        TEMP = 1.0
        EPS = 0.0001

        def _forward(x, gate_w, gate_b, value_w, geom_w, geom_b, pw_w, pw_b):
            Bb, C, Hh, Ww = x.shape
            L = Hh * Ww
            S = K * K
            pad = K // 2
            gate = jnp.einsum('bchw,rc->brhw', x, gate_w) + gate_b[None, :, None, None]
            mu = jax.nn.softmax(gate / TEMP, axis=1).reshape(Bb, R, 1, L)
            v = jnp.einsum('bchw,dc->bdhw', x, value_w)
            vp = jnp.pad(v, ((0, 0), (0, 0), (pad, pad), (pad, pad)))
            patches = jnp.stack([vp[:, :, i:i + Hh, j:j + Ww] for i in range(K) for j in range(K)], axis=2).reshape(Bb, C, S, L)
            g = jnp.einsum('bchw,gc->bghw', x, geom_w) + geom_b[None, :, None, None]
            g = g.reshape(Bb, 3, R, L)
            theta, raw_base, raw_hyp = (g[:, 0], g[:, 1], g[:, 2])
            base = jax.nn.softplus(raw_base) + EPS
            hyper = jax.nn.softplus(raw_hyp) + MIN_HYP
            sig_u = (base * jnp.exp(hyper))[:, :, None, :]
            sig_s = (base * jnp.exp(-hyper))[:, :, None, :]
            ct = jnp.cos(theta)[:, :, None, :]
            st = jnp.sin(theta)[:, :, None, :]
            offs = np.array([(r - pad, c - pad) for r in range(K) for c in range(K)], dtype=np.float32)
            dy = jnp.asarray(offs[:, 0]).reshape(1, 1, S, 1)
            dx = jnp.asarray(offs[:, 1]).reshape(1, 1, S, 1)
            pu = ct * dx + st * dy
            ps = -st * dx + ct * dy
            kern = jnp.exp(-(pu / sig_u) ** 2 - (ps / sig_s) ** 2)
            w = mu * kern
            w = w / (jnp.sum(w, axis=(1, 2), keepdims=True) + 1e-06)
            agg = jnp.einsum('brsl,bcsl->brcl', w, patches).reshape(Bb, R * C, Hh, Ww)
            return jnp.einsum('bkhw,ok->bohw', agg, pw_w) + pw_b[None, :, None, None]
        return _forward(x, gate_w, gate_b, value_w, geom_w, geom_b, pw_w, pw_b)

    def _L1_conv_ref(x, w1, w2, w3):
        import jax, jax.numpy as jnp
        import numpy as np
        DN = ('NCHW', 'OIHW', 'NCHW')

        def conv3x3(x, w):
            return jax.lax.conv_general_dilated(x, w, window_strides=(1, 1), padding=((1, 1), (1, 1)), dimension_numbers=DN)
        x = conv3x3(x, w1)
        x = conv3x3(x, w2)
        return conv3x3(x, w3)

    def _gn(v, G=32, eps=1e-05):
        B_, C_, H_, W_ = v.shape
        g = v.reshape(B_, G, C_ // G, H_, W_)
        m = jnp.mean(g, axis=(2, 3, 4), keepdims=True)
        s = jnp.var(g, axis=(2, 3, 4), keepdims=True)
        return ((g - m) / jnp.sqrt(s + eps)).reshape(v.shape)

    def _ln_c(v, eps=1e-06):
        m = jnp.mean(v, axis=1, keepdims=True)
        s = jnp.var(v, axis=1, keepdims=True)
        return (v - m) / jnp.sqrt(s + eps)

    def _ln_t(v, eps=1e-05):
        m = jnp.mean(v, axis=-1, keepdims=True)
        s = jnp.var(v, axis=-1, keepdims=True)
        return (v - m) / jnp.sqrt(s + eps)

    def _to_tokens(v):
        B_, C_, H_, W_ = v.shape
        return v.reshape(B_, C_, H_ * W_).transpose(0, 2, 1)

    def _from_tokens(t, like):
        B_, C_, H_, W_ = like.shape
        return t.transpose(0, 2, 1).reshape(B_, C_, H_, W_)
    x = x + _L0_conv_ref(_gn(x), L0_conv_gate_w, L0_conv_gate_b, L0_conv_value_w, L0_conv_geom_w, L0_conv_geom_b, L0_conv_pw_w, L0_conv_pw_b)
    x = x + _L1_conv_ref(_gn(x), L1_conv_w1, L1_conv_w2, L1_conv_w3)
    return x

_drawn_inputs = setup_inputs


def setup_inputs(seed=0):
    import zlib

    import numpy as np

    out = dict(_drawn_inputs(seed))
    spreads = {}
    factors = {'L0_conv_gate_w': 8.0,
     'L0_conv_gate_b': 38.27,
     'L0_conv_geom_w': 7.635,
     'L0_conv_geom_b': 55.307}
    for name, (base, spread) in spreads.items():
        noise = np.random.default_rng([zlib.crc32(name.encode()), seed]).standard_normal(out[name].shape)
        drawn = base * np.exp(spread * noise) if base else spread * noise
        out[name] = jnp.asarray(drawn.astype(out[name].dtype))
    for name, factor in factors.items():
        out[name] = (out[name] * factor).astype(out[name].dtype)
    return out
```

```python
from contextlib import ExitStack

import concourse.bass as bass
from concourse import mybir

F32 = mybir.dt.float32
F32R = mybir.dt.float32r
ALU = mybir.AluOpType
ACT = mybir.ActivationFunctionType
AX = mybir.AxisListType

P = 128
IMAGES, C, H, W = 8, 32, 64, 64
G = 4
QR = H // G
K8 = QR // 2
R = 4
TAPS = 5
MID = 64
PW = W + 2
GEO = G * 4 * R
NW = K8 * G * R
UNITS = 2 * TAPS
HALF = K8 // 2 * G * P
BANK = 512

EPS_GN = 1e-5
EPS_BASE = 1e-4
MIN_HYP = 0.1
EPS_Z = 1e-6
INV_2PI = 0.15915494309189535
TWO_PI_HI = 6.28125
TWO_PI_LO = 0.0019353071795864769
ROUND = 12582912.0
PI_BELOW = 3.1415925

UNIT_TAP = (1, 2, 3, 4, 0)
PROD_BUF = (0, 1, 2, 3, 4, 5, 6, 0, 1, 2)
N_PROD = 7

CHUNKS = ([(1, 8 * n, 8) for n in range(4)]
          + [(2, 0, 7), (2, 7, 7), (2, 14, 7), (2, 21, 6), (2, 27, 6)]
          + [(3, 0, 8), (3, 8, 8)])
N_SPLIT = 9
N_OUT = 2

GN1_V, GN2_V = 9, 11
CH_V, CH_A = 29, 12


def conv_l0_l1_kernel(nc, x, geo_w, geo_bias, val_w, pw_t, pw_b, w1, w2, w3, ident, sel_quarter,
                      sel_slots, masks, consts, out):
    ctx = ExitStack()
    with ctx:
        def sb(name, shape, dt=F32):
            return ctx.enter_context(nc.sbuf_tensor(name, shape, dt))

        def pb(name):
            return ctx.enter_context(nc.psum_tensor(name, [P, BANK], F32))

        def sem(name):
            return ctx.enter_context(nc.semaphore(name))

        geo_w_sb = sb("geo_w_sb", [P, GEO])
        geo_bias_sb = sb("geo_bias_sb", [P, GEO])
        val_w_sb = sb("val_w_sb", [P, P])
        pw_t_sb = sb("pw_t_sb", [P, C])
        pw_b_sb = sb("pw_b_sb", [P, 1])
        ident_sb = sb("ident_sb", [P, P])
        sel1_sb = sb("sel1_sb", [P, P])
        sel2_sb = sb("sel2_sb", [P, P])
        masks_sb = sb("masks_sb", [P, 3])
        consts_sb = sb("consts_sb", [P, 5])
        NC = (3 + 6 + 9) * P
        wc_hi = sb("wc_hi", [P, NC], F32R)
        wc_lo = sb("wc_lo", [P, NC], F32R)
        xraw = sb("xraw", [P, QR + 2, W])
        xkeep = sb("xkeep", [P, QR * W])
        xn = sb("xn", [P, QR + 2, PW])
        tap_x = sb("tap_x", [P, TAPS, QR, W])
        st1 = sb("st1", [P, 2, 6])
        mv1 = sb("mv1", [P, 2])
        gn1 = sb("gn1", [P, 16])
        geo = sb("geo", [P, 4, NW])
        ch = sb("ch", [P, 14, NW])
        trig = sb("trig", [P, 4, NW])
        trig2 = sb("trig2", [P, 4, NW])
        expo = sb("expo", [P, 2, 4, NW])
        small = sb("small", [P, 5, K8 * G])
        tapw = sb("tapw", [P, TAPS, NW])
        prod = sb("prod", [P, N_PROD, HALF])
        agg = sb("agg", [P, 2, BANK])
        x2 = sb("x2", [P, QR * W])
        x2q = sb("x2q", [P, H // 2, W])
        x2r = sb("x2r", [P, H // 4, W])
        st2 = sb("st2", [P, 4, 6])
        mv2 = sb("mv2", [P, 2])
        gn2 = sb("gn2", [P, 16])
        xq_hi = sb("xq_hi", [P, H // 2, PW], F32R)
        xq_lo = sb("xq_lo", [P, H // 2, PW], F32R)
        c1_hi = sb("c1_hi", [P, H // 2 + 2, PW], F32R)
        c1_lo = sb("c1_lo", [P, H // 2 + 2, PW], F32R)
        c2_hi = sb("c2_hi", [P, H // 2 + 1, PW], F32R)
        c2_lo = sb("c2_lo", [P, H // 2 + 1, PW], F32R)
        outb = sb("outb", [P, H // 4, W])

        geo_ps = pb("geo_ps")
        val_ps = [pb("val_ps0"), pb("val_ps1")]
        agg_ps = [pb("agg_ps0"), pb("agg_ps1")]
        pw_ps = pb("pw_ps")
        conv_ps = [pb("conv_ps0"), pb("conv_ps1")]

        consts_in = sem("consts_in")
        w_hi = sem("w_hi")
        w_lo = sem("w_lo")
        pads = sem("pads")
        edges = sem("edges")
        x_in = sem("x_in")
        x_kept = sem("x_kept")
        gn1_v = sem("gn1_v")
        gn1_pe = sem("gn1_pe")
        gn1_pow = sem("gn1_pow")
        xn_done = sem("xn_done")
        pairs_done = sem("pairs_done")
        geo_done = sem("geo_done")
        ch_v = sem("ch_v")
        ch_a = sem("ch_a")
        val_done = sem("val_done")
        mult_done = sem("mult_done")
        add_done = sem("add_done")
        agg_t = sem("agg_t")
        agg_sb = sem("agg_sb")
        pw_done = sem("pw_done")
        pw_each = sem("pw_each")
        x2_done = sem("x2_done")
        x2q_in = sem("x2q_in")
        x2r_in = sem("x2r_in")
        gn2_v = sem("gn2_v")
        gn2_pe = sem("gn2_pe")
        gn2_pow = sem("gn2_pow")
        xq_norm = sem("xq_norm")
        xq_hi_done = sem("xq_hi_done")
        xq_lo_done = sem("xq_lo_done")
        conv_done = sem("conv_done")
        hi_done = sem("hi_done")
        lo_done = sem("lo_done")
        out_done = sem("out_done")
        out_st = sem("out_st")

        def at(i, per_image, n):
            return per_image * i + n

        def sure(i, n=1):
            return not isinstance(i, int) or i >= n

        block = ctx.enter_context(nc.Block())
        NCONST = 10
        N_PADS = 7 * 2 + 2 * 2 + 2
        N_EDGES = 4 + 2 * 2

        def run_images(eng, body):
            body(0, True, False, True)
            with eng.Fori(1, IMAGES - 1) as i:
                body(i, True, True, True)
            body(IMAGES - 1, True, True, False)
            body(IMAGES, False, True, False)

        @block.sync
        def _(sp):
            def wait(s, v):
                sp.wait_ge(s, v)
                sp.nop(nofuse=True)

            def load_x(j):
                for g in range(G):
                    lo, hi = max(0, QR * g - 1), min(H, QR * g + QR + 1)
                    at0 = lo - (QR * g - 1)
                    sp.dma_start(xraw[C * g:C * g + C, at0:at0 + hi - lo, :], x[j, :, lo:hi, :]).then_inc(x_in, 16)

            def keep_x(j):
                sp.dma_start(xkeep[:, :], xraw[:, 1:QR + 1, :].rearrange("p r w -> p (r w)")).then_inc(x_kept, 16)

            def store(j, n):
                for s in range(4):
                    dst = out[j, :, :, :].rearrange("c (q s) w -> c q s w", s=4)[:, 8 * n:8 * n + 8, s, :]
                    sp.dma_start(dst, outb[C * s:C * s + C, 8 * n:8 * n + 8, :]).then_inc(out_st, 16)

            def body(i, back, conv, front):
                if front:
                    if back and sure(i, 0):
                        wait(xn_done, at(i, 2, 2))
                        wait(x_kept, at(i, 16, 16))
                    load_x(i + 1)
                if back:
                    wait(x2_done, at(i, 2, 2))
                    if sure(i):
                        wait(xq_lo_done, at(i, 1, 0))
                    x2v = x2[:, :].rearrange("p (r w) -> p r w", w=W)
                    for g in range(G):
                        src = x2v[C * g:C * g + C].rearrange("p (h t) w -> p t h w", t=2)
                        for s in range(4):
                            par, first = (1, 8 * g + 1) if s == 0 else (0, 8 * g) if s == 1 else \
                                         (1, 8 * g) if s == 2 else (0, 8 * g - 1)
                            a = 1 if first < 0 else 0
                            b = 7 if first + 8 > H // 2 else 8
                            sp.dma_start(x2q[C * s:C * s + C, first + a:first + b, :],
                                         src[:, par, a:b, :]).then_inc(x2q_in, 16)
                if front:
                    wait(x_in, at(i + 1, 64, 64))
                    keep_x(i + 1)
                if conv:
                    j = i - 1
                    for n in range(2):
                        wait(out_done, at(j, 2, n + 1))
                        store(j, n)
                if back:
                    if conv:
                        pass
                    for g in range(G):
                        src = x2v[C * g:C * g + C].rearrange("p (q s) w -> p s q w", s=4)
                        for s in range(4):
                            sp.dma_start(x2r[C * s:C * s + C, 4 * g:4 * g + 4, :],
                                         src[:, s]).then_inc(x2r_in, 16)

            for n, (dst, src) in enumerate([
                    (geo_w_sb, geo_w), (geo_bias_sb, geo_bias), (val_w_sb, val_w), (pw_t_sb, pw_t),
                    (pw_b_sb, pw_b), (ident_sb, ident), (sel1_sb, sel_quarter), (sel2_sb, sel_slots),
                    (masks_sb, masks), (consts_sb, consts)]):
                if n == 0:
                    load_x(0)
                sp.dma_start(dst[:, :], src).then_inc(consts_in, 16)
            wflat = prod[:, 0:2, :].rearrange("p n f -> p (n f)")
            for dst0, src, n in ((0, w1, 3), (3, w2, 6), (9, w3, 9)):
                sp.dma_start(wflat[:, dst0 * P:(dst0 + n) * P], src).then_inc(consts_in, 16)
            wait(x_in, 64)
            keep_x(0)
            run_images(sp, body)
            wait(out_st, 16 * 8 * IMAGES)

        ALL_CONST = 16 * (NCONST + 3)

        def conv_terms(n):
            layer, j0, m = CHUNKS[n]
            if layer == 1:
                for dx in range(3):
                    yield dx, xq_hi[:, j0:j0 + m, dx:dx + W], xq_lo[:, j0:j0 + m, dx:dx + W]
            if layer == 2:
                for t in range(2):
                    for dx in range(3):
                        yield (3 + 3 * t + dx, c1_hi[:, j0 + t:j0 + t + m, dx:dx + W],
                               c1_lo[:, j0 + t:j0 + t + m, dx:dx + W])
            if layer == 3:
                for t in range(3):
                    a, b = 2 * j0 + t, 2 * (j0 + m - 1) + t + 1
                    for dx in range(3):
                        yield 9 + 3 * t + dx, c2_hi[:, a:b:2, dx:dx + W], c2_lo[:, a:b:2, dx:dx + W]

        def conv_cols(n):
            return CHUNKS[n][2] * W

        def lo_needed(n):
            layer, j0, m = CHUNKS[n]
            if layer == 2:
                return min(4, (j0 + m - 1) // 8 + 1)
            return 9 if n == 10 else 4 + 3

        @block.tensor
        def _(pe):
            def conv_steps(j):
                for n in range(len(CHUNKS)):
                    if n == 0:
                        if sure(j):
                            pe.wait_ge(out_done, at(j, 2, 0))
                    elif 2 <= n < N_SPLIT + 2 and n - 2 < N_SPLIT:
                        pe.wait_ge(lo_done, at(j, N_SPLIT, n - 1))
                    if n == 0:
                        pe.wait_ge(xq_lo_done, at(j, 1, 1))
                    elif n >= 4:
                        pe.wait_ge(lo_done, at(j, N_SPLIT, lo_needed(n)))
                    terms = list(conv_terms(n))
                    dst = conv_ps[n % 2][:, 0:conv_cols(n)]
                    for m, (w, hi, lo) in enumerate(terms):
                        w_h, w_l = wc_hi[:, w * P:(w + 1) * P], wc_lo[:, w * P:(w + 1) * P]
                        last = m == len(terms) - 1
                        nc.tensor.matmul(dst, w_h, hi, start=m == 0, stop=False)
                        yield
                        nc.tensor.matmul(dst, w_h, lo, start=False, stop=False)
                        yield
                        mm = nc.tensor.matmul(dst, w_l, hi, start=False, stop=last)
                        if last:
                            mm.then_inc(conv_done, 1)
                        yield

            def values(i, u):
                if u >= 2 or sure(i):
                    pe.wait_ge(mult_done, at(i, UNITS, u - 1))
                h, tap = u // TAPS, UNIT_TAP[u % TAPS]
                if u == 0:
                    pe.wait_ge(pairs_done, at(i, 1, 1))
                for kk in range(K8 // 2):
                    k = h * K8 // 2 + kk
                    src = tap_x[:, tap, 2 * k:2 * k + 2, :].rearrange("p r w -> p (r w)")
                    mm = nc.tensor.matmul(val_ps[u % 2][:, kk * P:(kk + 1) * P], src, val_w_sb[:, :],
                                          start=kk == 0, stop=kk == K8 // 2 - 1, skip_group_check=True)
                mm.then_inc(val_done, 1)

            def transpose_sums(i, n):
                h, g = n // 4, n % 4
                if g == 0:
                    pe.wait_ge(mult_done, at(i, UNITS, 5 * h + 5))
                    pe.wait_ge(add_done, at(i, 4, 2 * h + 2))
                if n >= 2 or sure(i):
                    pe.wait_ge(agg_sb, at(i, 8, n - 1))
                bufs = [PROD_BUF[5 * h + q] for q in (4, 0, 2)]
                for kk in range(K8 // 2):
                    at0 = (kk * G + g) * P
                    for m, b in enumerate(bufs):
                        mm = nc.tensor.matmul(agg_ps[n % 2][:, kk * P:(kk + 1) * P], prod[:, b, at0:at0 + P],
                                              ident_sb[:, :], is_transpose=True, start=m == 0,
                                              stop=m == len(bufs) - 1)
                mm.then_inc(agg_t, 1)

            def pointwise(i, n):
                h, g = n // 4, n % 4
                if n == 0 and sure(i):
                    pe.wait_ge(gn2_v, at(i, GN2_V, 0))
                if g == 0 and (h or sure(i)):
                    pe.wait_ge(x2_done, at(i, 2, h))
                pe.wait_ge(agg_sb, at(i, 8, n + 1))
                mm = nc.tensor.matmul(pw_ps[C * g:C * g + C, :], pw_t_sb[:, :], agg[:, n % 2, :],
                                      start=True, stop=True)
                mm.then_inc(pw_each, 1)

            def gn_sum(sem_v, value, sel, src, dst, done):
                pe.wait_ge(sem_v, value)
                nc.tensor.matmul(dst, sel[:, :], src, start=True, stop=True).then_inc(done, 1)

            def geometry(i):
                pe.wait_ge(xn_done, at(i, 2, 1))
                for k in range(K8):
                    mm = nc.tensor.matmul(geo_ps[:, k * GEO:(k + 1) * GEO],
                                          tap_x[:, 0, 2 * k:2 * k + 2, :].rearrange("p r w -> p (r w)"),
                                          geo_w_sb[:, :],
                                          start=k == 0, stop=k == K8 - 1, skip_group_check=True)
                mm.then_inc(geo_done, 1)

            def gn1_sums(i, n):
                if n == 0:
                    if sure(i):
                        pe.wait_ge(ch_v, at(i - 1, CH_V, 1))
                    gn_sum(gn1_v, at(i, GN1_V, 3), sel1_sb, mv1[:, 0:1], geo_ps[:, 0:1], gn1_pe)
                else:
                    gn_sum(gn1_v, at(i, GN1_V, 6), sel1_sb, gn1[:, 2:3], geo_ps[:, 1:2], gn1_pe)

            def gn2_sums(i, n):
                if n == 0:
                    gn_sum(gn2_v, at(i, GN2_V, 5), sel2_sb, mv2[:, 0:1], pw_ps[:, 0:1], gn2_pe)
                else:
                    gn_sum(gn2_v, at(i, GN2_V, 8), sel2_sb, gn2[:, 2:3], pw_ps[:, 1:2], gn2_pe)

            def body(i, back, conv, front):
                steps = conv_steps(i - 1) if conv else iter(())

                def convs(n):
                    for _ in range(n):
                        next(steps, None)

                if back:
                    for u in range(UNITS):
                        values(i, u)
                        convs((4, 5, 5, 5, 5, 5, 5, 4, 4, 4)[u])
                        if front and u == 4:
                            gn1_sums(i + 1, 0)
                        if front and u == 5:
                            gn1_sums(i + 1, 1)
                        if u == 6:
                            transpose_sums(i, 0)
                            transpose_sums(i, 1)
                            convs(2)
                            transpose_sums(i, 2)
                            pointwise(i, 0)
                            transpose_sums(i, 3)
                            pointwise(i, 1)
                        if u == 7:
                            pointwise(i, 2)
                            pointwise(i, 3)
                if front:
                    geometry(i + 1)
                if back:
                    convs(12)
                    transpose_sums(i, 4)
                    transpose_sums(i, 5)
                    convs(2)
                    for n in (4, 5):
                        transpose_sums(i, n + 2)
                        pointwise(i, n)
                    convs(2)
                    pointwise(i, 6)
                    pointwise(i, 7)
                    convs(60)
                    gn2_sums(i, 0)
                    convs(6)
                    gn2_sums(i, 1)
                for _ in steps:
                    pass

            pe.wait_ge(consts_in, ALL_CONST)
            gn1_sums(0, 0)
            gn1_sums(0, 1)
            pe.wait_ge(pads, N_PADS)
            pe.wait_ge(edges, N_EDGES)
            geometry(0)
            pe.wait_ge(w_lo, 1)
            run_images(pe, body)

        @block.vector
        def _(dve):
            v = nc.vector

            def lo_region(n):
                layer, j0, m = CHUNKS[n]
                ps = conv_ps[n % 2][:, 0:conv_cols(n)].rearrange("p (j w) -> p j w", w=W)
                if layer == 1:
                    sl = slice(1 + j0, 1 + j0 + m)
                    return [(ps, c1_hi[:, sl, 1:1 + W], c1_lo[:, sl, 1:1 + W])]
                half = [(0, P, 0, m)]
                if j0 == 0:
                    half = [(MID, P, 0, 1), (0, P, 1, m)]
                if j0 + m == H // 2 + 1:
                    half = [(0, MID, m - 1, m), (0, P, 0, m - 1)]
                return [(ps[a:b, s:e], c2_hi[a:b, j0 + s:j0 + e, 1:1 + W], c2_lo[a:b, j0 + s:j0 + e, 1:1 + W])
                        for a, b, s, e in half]

            def low_part(j, n):
                dve.wait_ge(hi_done, at(j, N_SPLIT, n + 1))
                for ps, hi, lo in lo_region(n):
                    op = v.tensor_tensor(lo, ps, hi.bitcast(F32), ALU.subtract)
                op.then_inc(lo_done, 1)

            def result(j, n):
                dve.wait_ge(conv_done, at(j, len(CHUNKS), N_SPLIT + n + 1))
                if n == 0:
                    dve.wait_ge(x2r_in, at(j, 256, 256))
                    if sure(j):
                        dve.wait_ge(out_st, at(j, 128, 0))
                ps = conv_ps[(N_SPLIT + n) % 2][:, :].rearrange("p (j w) -> p j w", w=W)
                v.tensor_tensor(outb[:, 8 * n:8 * n + 8, :], ps, x2r[:, 8 * n:8 * n + 8, :],
                                ALU.add).then_inc(out_done, 1)

            def mult(i, u):
                h, tap = u // TAPS, UNIT_TAP[u % TAPS]
                dve.wait_ge(val_done, at(i, UNITS, u + 1))
                if u == 0:
                    dve.wait_ge(ch_v, at(i, CH_V, 29))
                    if sure(i):
                        dve.wait_ge(agg_t, at(i, 8, 0))
                if u == 7:
                    dve.wait_ge(agg_t, at(i, 8, 4))
                B = K8 // 2 * G
                val = val_ps[u % 2][:, :].rearrange("p (b c) -> p b c", c=C)
                wgt = tapw[:, tap, h * B * R:(h + 1) * B * R].rearrange("p (b r) -> p b r", r=R)
                dst = prod[:, PROD_BUF[u], :].rearrange("p (b r c) -> p b r c", r=R, c=C)
                v.tensor_tensor(dst, val.unsqueeze(2).to_broadcast([P, B, R, C]),
                                wgt.unsqueeze(3).to_broadcast([P, B, R, C]), ALU.mult).then_inc(mult_done, 1)

            def residual(i, h):
                dve.wait_ge(pw_each, at(i, 8, 4 * h + 4))
                if h == 0:
                    dve.wait_ge(x_kept, at(i, 16, 16))
                    if sure(i):
                        dve.wait_ge(x2r_in, at(i, 256, 0))
                        dve.wait_ge(x2q_in, at(i, 16 * 16, 0))
                sl = slice(h * BANK, (h + 1) * BANK)
                v.scalar_tensor_tensor(x2[:, sl], pw_ps[:, :], pw_b_sb[:, 0:1], xkeep[:, sl],
                                       ALU.add, ALU.add).then_inc(x2_done, 1)

            def stats(i, rows, st, mv, sv, per, src):
                for n in range(rows):
                    v.bn_stats(st[:, n, :], src(n)).then_inc(sv, 1)
                dve.wait_ge(sv, at(i, per, rows))
                dve.nop(nofuse=True)
                v.bn_aggr(mv[:, :], st[:, 0:rows, :].rearrange("p a b -> p (a b)")).then_inc(sv, 1)

            def gn_spread(i, sv, base, per, mv, t, ps, pe_sem):
                dve.wait_ge(pe_sem, at(i, 2, 1))
                v.tensor_copy(t[:, 0:1], ps[:, 0:1]).then_inc(sv, 1)
                v.tensor_tensor(t[:, 1:2], mv[:, 0:1], ps[:, 0:1], ALU.subtract).then_inc(sv, 1)
                dve.wait_ge(sv, at(i, per, base + 2))
                v.scalar_tensor_tensor(t[:, 2:3], t[:, 1:2], t[:, 1:2], mv[:, 1:2],
                                       ALU.mult, ALU.add).then_inc(sv, 1)

            def gn_eps(i, sv, per, t, ps, pe_sem):
                dve.wait_ge(pe_sem, at(i, 2, 2))
                v.tensor_scalar(t[:, 3:4], ps[:, 1:2], EPS_GN, None, ALU.add).then_inc(sv, 1)

            def gn_scale(i, sv, base, per, t, pow_sem):
                dve.wait_ge(pow_sem, at(i, 1, 1))
                v.tensor_scalar(t[:, 6:9], masks_sb[:, :], t[:, 4:5], None, ALU.mult)\
                    .then_inc(sv, 1)
                dve.wait_ge(sv, at(i, per, base + 1))
                v.tensor_scalar(t[:, 9:12], t[:, 6:9], t[:, 0:1], -1.0, ALU.mult, ALU.mult).then_inc(sv, 1)

            def gn1_a(i):
                dve.wait_ge(x_in, at(i, 64, 64))
                stats(i, 2, st1, mv1, gn1_v, GN1_V, lambda n: xraw[:, 1 + 8 * n:9 + 8 * n, :].rearrange("p r w -> p (r w)"))

            def gn1_b(i):
                gn_spread(i, gn1_v, 3, GN1_V, mv1, gn1, geo_ps, gn1_pe)

            def gn1_c(i):
                gn_eps(i, gn1_v, GN1_V, gn1, geo_ps, gn1_pe)

            def gn1_d(i):
                gn_scale(i, gn1_v, 7, GN1_V, gn1, gn1_pow)

            def link(i, s, per, k, op):
                op.then_inc(s, 1)
                dve.wait_ge(s, at(i, per, k))

            def chain(i):
                gate, theta = geo[:, 0, :], geo[:, 1, :]
                raw = geo[:, 2:4, :]
                e, gs = ch[:, 0, :], ch[:, 1, :]
                th, kk, th2 = ch[:, 2, :], ch[:, 3, :], ch[:, 4, :]
                t, w = ch[:, 6:8, :], ch[:, 8:10, :]
                l, spl = ch[:, 10:12, :], ch[:, 12:14, :]

                def step(k, op):
                    link(i, ch_v, CH_V, k, op)

                def need_act(k):
                    dve.wait_ge(ch_a, at(i, CH_A, k))

                dve.wait_ge(geo_done, at(i, 1, 1))
                src = geo_ps[:, :].rearrange("p (k q j) -> p q k j", q=4, j=G * R)
                bias = geo_bias_sb[:, :].rearrange("p (q j) -> p q j", q=4).unsqueeze(2)\
                    .to_broadcast([P, 4, K8, G * R])
                step(1, v.tensor_tensor(geo[:, :, :].rearrange("p q (k j) -> p q k j", j=G * R), src, bias, ALU.add))
                step(2, v.tensor_scalar(kk, theta, INV_2PI, ROUND, ALU.mult, ALU.add))
                step(3, v.tensor_scalar(kk, kk, -ROUND, None, ALU.add))
                step(4, v.scalar_tensor_tensor(th, kk, -TWO_PI_HI, theta, ALU.mult, ALU.add))
                step(5, v.scalar_tensor_tensor(th, kk, -TWO_PI_LO, th, ALU.mult, ALU.add))
                step(6, v.tensor_scalar(th2, th, PI_BELOW, -PI_BELOW, ALU.min, ALU.max))
                g4 = gate.rearrange("p (b r) -> p b r", r=R)
                step(7, v.tensor_reduce(small[:, 0, :], g4, AX.X, ALU.max))
                step(8, v.tensor_tensor(gs.rearrange("p (b r) -> p b r", r=R), g4,
                                        small[:, 0, :].unsqueeze(2).to_broadcast([P, K8 * G, R]), ALU.subtract))
                need_act(3)
                step(9, v.tensor_tensor(trig[:, 2, :], trig[:, 0, :], trig[:, 1, :], ALU.add))
                step(10, v.tensor_tensor(trig[:, 3, :], trig[:, 0, :], trig[:, 1, :], ALU.subtract))
                need_act(6)
                step(11, v.tensor_scalar(w, t, 1.0, None, ALU.add))
                step(12, v.scalar_tensor_tensor(t, w, -1.0, t, ALU.add, ALU.subtract))
                need_act(8)
                step(13, v.tensor_tensor(l, l, t, ALU.subtract))
                step(14, v.scalar_tensor_tensor(spl, raw, 0.0, l, ALU.max, ALU.add))
                need_act(9)
                step(15, v.tensor_tensor(w[:, 0, :], spl[:, 1, :], gs, ALU.add))
                step(16, v.tensor_tensor(w[:, 1, :], spl[:, 1, :], gs, ALU.subtract))
                need_act(11)
                sq = trig2[:, :, :]
                step(17, v.tensor_tensor(expo[:, 0], sq, t[:, 0, :].unsqueeze(1).to_broadcast([P, 4, NW]), ALU.mult))
                step(18, v.tensor_tensor(expo[:, 1], sq, t[:, 1, :].unsqueeze(1).to_broadcast([P, 4, NW]), ALU.mult))
                ea = expo[:, 0].rearrange("p (h w) n -> p h w n", w=2)
                eb = expo[:, 1].rearrange("p (h w) n -> p h w n", w=2)
                step(19, v.tensor_tensor(ea[:, :, 0], ea[:, :, 0], eb[:, :, 1], ALU.add))
                step(20, v.tensor_tensor(ea[:, :, 1], ea[:, :, 1], eb[:, :, 0], ALU.add))
                need_act(12)
                kern = trig[:, :, :]
                step(21, v.tensor_reduce(kk, kern.rearrange("p t n -> p n t"), AX.X, ALU.add))
                step(22, v.tensor_scalar(kk, kk, 2.0, 1.0, ALU.mult, ALU.add))
                step(23, v.tensor_tensor(kk, kk, e, ALU.mult))
                step(24, v.tensor_reduce(small[:, 1, :], kk.rearrange("p (b r) -> p b r", r=R), AX.X, ALU.add))
                step(25, v.tensor_reduce(small[:, 2, :], e.rearrange("p (b r) -> p b r", r=R), AX.X, ALU.add))
                step(26, v.scalar_tensor_tensor(small[:, 3, :], small[:, 2, :], EPS_Z, small[:, 1, :],
                                                ALU.mult, ALU.add))
                step(27, v.reciprocal(small[:, 4, :], small[:, 3, :]))
                step(28, v.tensor_tensor(tapw[:, 0, :].rearrange("p (b r) -> p b r", r=R),
                                         e.rearrange("p (b r) -> p b r", r=R),
                                         small[:, 4, :].unsqueeze(2).to_broadcast([P, K8 * G, R]), ALU.mult))
                step(29, v.tensor_tensor(tapw[:, 1:TAPS, :], kern,
                                         tapw[:, 0, :].unsqueeze(1).to_broadcast([P, 4, NW]), ALU.mult))

            def gn2_a(i):
                dve.wait_ge(x2q_in, at(i, 256, 256))
                stats(i, 4, st2, mv2, gn2_v, GN2_V, lambda n: x2q[:, 8 * n:8 * n + 8, :].rearrange("p r w -> p (r w)"))

            def split_low(i):
                dve.wait_ge(xq_hi_done, at(i, 1, 1))
                v.tensor_tensor(xq_lo[:, :, 1:1 + W], x2q[:, :, :], xq_hi[:, :, 1:1 + W].bitcast(F32),
                                ALU.subtract).then_inc(xq_lo_done, 1)

            def body(i, back, conv, front):
                j = i - 1
                if back:
                    for u in range(UNITS):
                        mult(i, u)
                        if front and u == 1:
                            gn1_a(i + 1)
                        if conv and u in (2, 4, 6, 8):
                            low_part(j, u // 2 - 1)
                        if front and u == 5:
                            gn1_b(i + 1)
                        if front and u == 6:
                            gn1_c(i + 1)
                        if front and u == 7:
                            gn1_d(i + 1)
                    residual(i, 0)
                else:
                    for n in range(4):
                        low_part(j, n)
                if front:
                    chain(i + 1)
                if conv:
                    low_part(j, 4)
                if back:
                    residual(i, 1)
                if conv:
                    low_part(j, 5)
                    low_part(j, 6)
                if back:
                    gn2_a(i)
                    gn_spread(i, gn2_v, 5, GN2_V, mv2, gn2, pw_ps, gn2_pe)
                if conv:
                    low_part(j, 7)
                if back:
                    gn_eps(i, gn2_v, GN2_V, gn2, pw_ps, gn2_pe)
                    gn_scale(i, gn2_v, 9, GN2_V, gn2, gn2_pow)
                if conv:
                    low_part(j, 8)
                    result(j, 0)
                if back:
                    split_low(i)
                if conv:
                    result(j, 1)

            for rows in (xraw[0:C, 0, :], xraw[3 * C:P, QR + 1, :], x2q[0:C, 0, :], x2q[3 * C:P, H // 2 - 1, :]):
                v.memset(rows, 0.0).then_inc(edges, 1)
            for tile in (c2_hi, c2_lo):
                v.memset(tile[0:MID, 0, 1:1 + W].bitcast(F32), 0.0).then_inc(edges, 1)
                v.memset(tile[MID:P, H // 2, 1:1 + W].bitcast(F32), 0.0).then_inc(edges, 1)
            dve.wait_ge(consts_in, ALL_CONST)
            gn1_a(0)
            gn1_b(0)
            gn1_c(0)
            gn1_d(0)
            dve.wait_ge(w_hi, 1)
            v.tensor_tensor(wc_lo[:, :], prod[:, 0:2, :].rearrange("p n f -> p (n f)")[:, 0:NC],
                            wc_hi[:, :].bitcast(F32), ALU.subtract).then_inc(w_lo, 1)
            dve.wait_ge(w_lo, 1)
            chain(0)
            run_images(dve, body)

        @block.scalar
        def _(act):
            s = nc.scalar
            C_PI2, C_EPSB, C_MH, C_PH, C_ONE = (consts_sb[:, k:k + 1] for k in range(5))

            def hi_part(j, n):
                act.wait_ge(conv_done, at(j, len(CHUNKS), n + 1))
                layer, j0, m = CHUNKS[n]
                ps = conv_ps[n % 2][:, 0:conv_cols(n)].rearrange("p (j w) -> p j w", w=W)
                if layer == 1:
                    parts = [(ps, c1_hi[:, 1 + j0:1 + j0 + m, 1:1 + W])]
                else:
                    half = [(0, P, 0, m)]
                    if j0 == 0:
                        half = [(MID, P, 0, 1), (0, P, 1, m)]
                    if j0 + m == H // 2 + 1:
                        half = [(0, MID, m - 1, m), (0, P, 0, m - 1)]
                    parts = [(ps[a:b, q:r], c2_hi[a:b, j0 + q:j0 + r, 1:1 + W]) for a, b, q, r in half]
                for src, dst in parts:
                    op = s.activation(dst, src, ACT.Copy)
                op.then_inc(hi_done, 1)

            def sums_out(i, n):
                act.wait_ge(agg_t, at(i, 8, n + 1))
                if n >= 2 or sure(i):
                    act.wait_ge(pw_each, at(i, 8, n - 1))
                s.activation(agg[:, n % 2, :], agg_ps[n % 2][:, :], ACT.Copy).then_inc(agg_sb, 1)

            def norm1(i):
                act.wait_ge(gn1_v, at(i, GN1_V, GN1_V))
                if sure(i):
                    act.wait_ge(val_done, at(i, UNITS, 0))
                    act.wait_ge(pairs_done, at(i, 1, 0))
                s.activation(tap_x[:, 0], xraw[:, 1:QR + 1, :], ACT.Identity,
                             scale=gn1[:, 6:7], bias=gn1[:, 9:10]).then_inc(xn_done, 1)
                for row, n, m in ((0, 1, 1), (QR + 1, 1, 2), (1, QR, 0)):
                    op = s.activation(xn[:, row:row + n, 1:1 + W], xraw[:, row:row + n, :], ACT.Identity,
                                      scale=gn1[:, 6 + m:7 + m], bias=gn1[:, 9 + m:10 + m])
                op.then_inc(xn_done, 1)

            def chain(i):
                gs = ch[:, 1, :]
                th2, tha = ch[:, 4, :], ch[:, 5, :]
                t, w, l, spl = ch[:, 6:8, :], ch[:, 8:10, :], ch[:, 10:12, :], ch[:, 12:14, :]

                def need(k):
                    act.wait_ge(ch_v, at(i, CH_V, k))

                def step(k, op):
                    op.then_inc(ch_a, 1)
                    act.wait_ge(ch_a, at(i, CH_A, k))

                need(6)
                step(1, s.activation(tha, th2, ACT.Abs))
                step(2, s.activation(trig[:, 1, :], th2, ACT.Sin))
                step(3, s.activation(trig[:, 0, :], tha, ACT.Sin, scale=-1.0, bias=C_PI2))
                need(8)
                step(4, s.activation(ch[:, 0, :], gs, ACT.Exp))
                step(5, s.activation(t, geo[:, 2:4, :], ACT.Abs))
                step(6, s.activation(t, t, ACT.Exp, scale=-1.0))
                need(10)
                step(7, s.activation(trig2[:, :, :], trig[:, :, :], ACT.Square))
                need(12)
                step(8, s.activation(l, w, ACT.Ln))
                need(14)
                step(9, s.activation(gs, spl[:, 0, :], ACT.Ln, bias=C_EPSB))
                need(16)
                step(10, s.activation(t[:, 0, :], w[:, 0, :], ACT.Exp, scale=-2.0, bias=C_MH))
                step(11, s.activation(t[:, 1, :], w[:, 1, :], ACT.Exp, scale=2.0, bias=C_PH))
                need(20)
                step(12, s.activation(trig[:, :, :], expo[:, 0], ACT.Exp, scale=-1.0))

            def norm2(i):
                act.wait_ge(gn2_v, at(i, GN2_V, GN2_V + 0))
                for row, n, m in ((0, 1, 1), (H // 2 - 1, 1, 2), (1, H // 2 - 2, 0)):
                    op = s.activation(x2q[:, row:row + n, :], x2q[:, row:row + n, :], ACT.Identity,
                                      scale=gn2[:, 6 + m:7 + m], bias=gn2[:, 9 + m:10 + m])
                op.then_inc(xq_norm, 1)

            def split_high(i):
                act.wait_ge(xq_norm, at(i, 1, 1))
                if sure(i):
                    act.wait_ge(conv_done, at(i - 1, len(CHUNKS), 4))
                s.activation(xq_hi[:, :, 1:1 + W], x2q[:, :, :], ACT.Copy).then_inc(xq_hi_done, 1)

            def body(i, back, conv, front):
                j = i - 1
                if conv:
                    for n in range(3):
                        hi_part(j, n)
                if back:
                    for n in range(4):
                        sums_out(i, n)
                if conv:
                    hi_part(j, 3)
                if front:
                    norm1(i + 1)
                    chain(i + 1)
                if conv:
                    hi_part(j, 4)
                if back:
                    for n in range(4, 8):
                        sums_out(i, n)
                if conv:
                    hi_part(j, 5)
                    hi_part(j, 6)
                    hi_part(j, 7)
                    hi_part(j, 8)
                if back:
                    norm2(i)
                    split_high(i)

            act.wait_ge(consts_in, ALL_CONST)
            s.activation(wc_hi[:, :], prod[:, 0:2, :].rearrange("p n f -> p (n f)")[:, 0:NC], ACT.Copy)\
                .then_inc(w_hi, 1)
            act.wait_ge(edges, N_EDGES)
            norm1(0)
            chain(0)
            run_images(act, body)

        @block.gpsimd
        def _(pool):
            p = nc.gpsimd

            def rstd(i, t, sv, per, n, done):
                pool.wait_ge(sv, at(i, per, n))
                p.tensor_tensor(t[:, 4:5], t[:, 3:4], t[:, 5:6], ALU.pow).then_inc(done, 1)

            def add_pair(i, n):
                u = 5 * (n // 2) + 2 * (n % 2)
                pool.wait_ge(mult_done, at(i, UNITS, u + 2))
                a, b = PROD_BUF[u], PROD_BUF[u + 1]
                p.tensor_tensor(prod[:, a, :], prod[:, a, :], prod[:, b, :], ALU.add).then_inc(add_done, 1)

            def shifted_sums(i):
                pool.wait_ge(xn_done, at(i, 2, 2))
                up, mid, down = slice(0, QR), slice(1, QR + 1), slice(2, QR + 2)
                left, here, right = slice(0, W), slice(1, 1 + W), slice(2, 2 + W)
                for n, (a, b) in enumerate((((mid, left), (mid, right)), ((up, here), (down, here)),
                                            ((up, left), (down, right)), ((up, right), (down, left)))):
                    op = p.tensor_tensor(tap_x[:, 1 + n], xn[:, a[0], a[1]], xn[:, b[0], b[1]], ALU.add)
                op.then_inc(pairs_done, 1)

            def body(i, back, conv, front):
                if back:
                    add_pair(i, 0)
                    add_pair(i, 1)
                    if front:
                        rstd(i + 1, gn1, gn1_v, GN1_V, 7, gn1_pow)
                    add_pair(i, 2)
                    add_pair(i, 3)
                if front:
                    if sure(i, 0):
                        pool.wait_ge(val_done, at(i, UNITS, UNITS))
                    shifted_sums(i + 1)
                if back:
                    rstd(i, gn2, gn2_v, GN2_V, 9, gn2_pow)

            for tile in (xn, xq_hi, xq_lo, c1_hi, c1_lo, c2_hi, c2_lo):
                for col in (0, PW - 1):
                    p.memset(tile[:, :, col:col + 1].bitcast(F32), 0.0).then_inc(pads, 1)
            for tile in (c1_hi, c1_lo):
                for row in (0, H // 2 + 1):
                    p.memset(tile[:, row, 1:1 + W].bitcast(F32), 0.0).then_inc(pads, 1)
            p.memset(gn1[:, 5:6], -0.5).then_inc(pads, 1)
            p.memset(gn2[:, 5:6], -0.5).then_inc(pads, 1)
            pool.wait_ge(pads, N_PADS)
            rstd(0, gn1, gn1_v, GN1_V, 7, gn1_pow)
            shifted_sums(0)
            run_images(pool, body)


def kernel(**inputs):
    import numpy as np
    import concourse.bacc as bacc
    from concourse import mybir as mb
    from concourse.bass_utils import run_bass_kernel_spmd

    a = {k: np.asarray(v) for k, v in inputs.items()}
    f = np.float32
    rows = np.concatenate([a["L0_conv_gate_w"], a["L0_conv_geom_w"]], axis=0).reshape(4, R, C)
    bias = np.concatenate([a["L0_conv_gate_b"], a["L0_conv_geom_b"]], axis=0).reshape(4, R)
    geo_w = np.zeros((G, C, 4, G, R), f)
    geo_bias = np.zeros((P, 4, G, R), f)
    val_w = np.zeros((G, C, G, C), f)
    for g in range(G):
        geo_w[g, :, :, g, :] = rows.transpose(2, 0, 1)
        geo_bias[:, :, g, :] = bias
        val_w[g, :, g, :] = a["L0_conv_value_w"].T
    pw_b = np.zeros((G, C, 1), f)
    pw_b[:, :, 0] = a["L0_conv_pw_b"]

    def banded(w, rows_in, rows_out, groups, step):
        o, c = w.shape[:2]
        m = np.zeros((rows_in, c, groups, 3, rows_out, o), f)
        for t in range(groups):
            for ri in range(rows_in):
                for ro in range(rows_out):
                    ky = step * t + ri - ro
                    if 0 <= ky <= 2:
                        m[ri, :, t, :, ro, :] = w[:, :, ky, :].transpose(1, 2, 0)
        return m.reshape(rows_in * c, groups * 3 * rows_out * o)

    sel_quarter = np.zeros((G, C, G, C), f)
    sel_slots = np.zeros((4, C, 4, C), f)
    for c in range(C):
        sel_quarter[:, c, :, c] = 1.0 / G
        sel_slots[1:3, c, :, c] = 0.5
    masks = np.ones((P, 3), f)
    masks[0:C, 1] = 0.0
    masks[P - C:P, 2] = 0.0
    consts = np.zeros((P, 5), f)
    consts[:, :] = np.array([1.5707963267948966, EPS_BASE, -2 * MIN_HYP, 2 * MIN_HYP, 1.0], f)
    arrays = {
        "x": np.ascontiguousarray(a["x"]), "geo_w": geo_w.reshape(P, GEO), "geo_bias": geo_bias.reshape(P, GEO),
        "val_w": val_w.reshape(P, P), "pw_t": np.ascontiguousarray(a["L0_conv_pw_w"].T), "pw_b": pw_b.reshape(P, 1),
        "w1": banded(a["L1_conv_w1"], 4, 2, 1, 0), "w2": banded(a["L1_conv_w2"], 2, 2, 2, 2),
        "w3": banded(a["L1_conv_w3"], 2, 4, 3, 2), "ident": np.eye(P, dtype=f),
        "sel_quarter": sel_quarter.reshape(P, P), "sel_slots": sel_slots.reshape(P, P),
        "masks": masks, "consts": consts,
    }
    nc = bacc.Bacc("TRN2", target_bir_lowering=False, num_devices=1)
    args = [nc.dram_tensor(f"in_{k}", v.shape, mb.dt.from_np(v.dtype), kind="ExternalInput").ap()
            for k, v in arrays.items()]
    out = nc.dram_tensor("out_y", (IMAGES, C, H, W), F32, kind="ExternalOutput").ap()
    conv_l0_l1_kernel(nc, *args, out)
    r = run_bass_kernel_spmd(nc, [{f"in_{k}": v for k, v in arrays.items()}], core_ids=[0])
    return r.results[0]["out_y"]
```

```python
from contextlib import ExitStack

import concourse.bass as bass
from concourse import mybir

F32 = mybir.dt.float32
F32R = mybir.dt.float32r
ALU = mybir.AluOpType
ACT = mybir.ActivationFunctionType
AX = mybir.AxisListType

P = 128
IMAGES, C, H, W = 8, 32, 64, 64
G = 4
QR = H // G
K8 = QR // 2
R = 4
TAPS = 5
MID = 64
PW = W + 2
GEO = G * 4 * R
NW = K8 * G * R
UNITS = 2 * TAPS
HALF = K8 // 2 * G * P
BANK = 512

EXP_SET = "natural_log_exp_and_others"

EPS_GN = 1e-5
EPS_BASE = 1e-4
MIN_HYP = 0.1
EPS_Z = 1e-6
INV_2PI = 0.15915494309189535
TWO_PI_HI = 6.28125
TWO_PI_LO = 0.0019353071795864769
ROUND = 12582912.0
PI_BELOW = 3.1415925

UNIT_TAP = (1, 2, 3, 4, 0)
PROD_BUF = (0, 1, 2, 3, 4, 5, 6, 1, 3, 2)
N_PROD = 7

CHUNKS = ([(1, 8 * n, 8) for n in range(4)]
          + [(2, 0, 7), (2, 7, 7), (2, 14, 7), (2, 21, 6), (2, 27, 6)]
          + [(3, 0, 8), (3, 8, 8)])
N_SPLIT = 9
N_OUT = 2

GN_V = 9
ADDS = 3
CH_V, CH_A = 29, 12


def conv_l0_l1_kernel(nc, x, geo_w, geo_bias, val_w, pw_t, pw_b, w1, w2, w3, ident, sel_quarter,
                      masks, consts, out):
    ctx = ExitStack()
    with ctx:
        def sb(name, shape, dt=F32):
            return ctx.enter_context(nc.sbuf_tensor(name, shape, dt))

        def pb(name):
            return ctx.enter_context(nc.psum_tensor(name, [P, BANK], F32))

        def sem(name):
            return ctx.enter_context(nc.semaphore(name))

        geo_w_sb = sb("geo_w_sb", [P, GEO])
        geo_bias_sb = sb("geo_bias_sb", [P, GEO])
        val_w_sb = sb("val_w_sb", [P, P])
        pw_t_sb = sb("pw_t_sb", [P, C])
        pw_b_sb = sb("pw_b_sb", [P, 1])
        ident_sb = sb("ident_sb", [P, P])
        sel1_sb = sb("sel1_sb", [P, P])
        masks_sb = sb("masks_sb", [P, 3])
        consts_sb = sb("consts_sb", [P, 5])
        NC = (3 + 6 + 9) * P
        wc_hi = sb("wc_hi", [P, NC], F32R)
        wc_lo = sb("wc_lo", [P, NC], F32R)
        xraw = sb("xraw", [P, QR + 2, W])
        xkeep = sb("xkeep", [P, QR * W])
        xn = sb("xn", [P, QR + 2, PW])
        tap_x = sb("tap_x", [P, TAPS, QR, W])
        st1 = sb("st1", [P, 2, 6])
        mv1 = sb("mv1", [P, 2])
        gn1 = sb("gn1", [P, 16])
        geo = sb("geo", [P, 4, NW])
        ch = sb("ch", [P, 15, NW])
        trig = sb("trig", [P, 4, NW])
        trig2 = sb("trig2", [P, 4, NW])
        expo = sb("expo", [P, 4, NW])
        small = sb("small", [P, 5, K8 * G])
        tapw = sb("tapw", [P, TAPS, NW])
        prod = sb("prod", [P, N_PROD, HALF])
        agg = sb("agg", [P, 2, BANK])
        x2 = sb("x2", [P, 2, QR // 2, W])
        x2s = sb("x2s", [P, 4, QR // 4, W])
        x2q = sb("x2q", [P, H // 2 + 2, W])
        x2r = sb("x2r", [P, H // 4, W])
        st2 = sb("st2", [P, 2, 6])
        mv2 = sb("mv2", [P, 2])
        gn2 = sb("gn2", [P, 16])
        xq_hi = sb("xq_hi", [P, H // 2, PW], F32R)
        xq_lo = sb("xq_lo", [P, H // 2, PW], F32R)
        c1_hi = sb("c1_hi", [P, H // 2 + 2, PW], F32R)
        c1_lo = sb("c1_lo", [P, H // 2 + 2, PW], F32R)
        c2_hi = sb("c2_hi", [P, H // 2 + 1, PW], F32R)
        c2_lo = sb("c2_lo", [P, H // 2 + 1, PW], F32R)

        geo_ps = pb("geo_ps")
        val_ps = [pb("val_ps0"), pb("val_ps1")]
        agg_ps = [pb("agg_ps0"), pb("agg_ps1")]
        pw_ps = pb("pw_ps")
        conv_ps = [pb("conv_ps0"), pb("conv_ps1")]

        consts_in = sem("consts_in")
        w_hi = sem("w_hi")
        w_lo = sem("w_lo")
        pads = sem("pads")
        edges = sem("edges")
        x_in = sem("x_in")
        x_kept = sem("x_kept")
        gn1_v = sem("gn1_v")
        gn1_pe = sem("gn1_pe")
        gn1_pow = sem("gn1_pow")
        xn_done = sem("xn_done")
        pairs_done = sem("pairs_done")
        geo_done = sem("geo_done")
        ch_v = sem("ch_v")
        ch_a = sem("ch_a")
        val_done = sem("val_done")
        mult_done = sem("mult_done")
        add_done = sem("add_done")
        agg_t = sem("agg_t")
        agg_sb = sem("agg_sb")
        pw_done = sem("pw_done")
        pw_each = sem("pw_each")
        x2_part = sem("x2_part")
        x2q_in = sem("x2q_in")
        x2r_in = sem("x2r_in")
        gn2_v = sem("gn2_v")
        gn2_pe = sem("gn2_pe")
        gn2_pow = sem("gn2_pow")
        x2s_done = sem("x2s_done")
        xq_act = sem("xq_act")
        xq_lo_done = sem("xq_lo_done")
        conv_done = sem("conv_done")
        hi_done = sem("hi_done")
        lo_done = sem("lo_done")
        out_done = sem("out_done")
        out_st = sem("out_st")

        def at(i, per_image, n):
            return per_image * i + n

        def sure(i, n=1):
            return not isinstance(i, int) or i >= n

        block = ctx.enter_context(nc.Block())
        NCONST = 9
        N_PADS = 7 * 2 + 2 * 2 + 2
        N_EDGES = 4 + 2 * 2

        def run_images(eng, body):
            body(0, True, False, True)
            body(1, True, True, True)
            with eng.Fori(2, IMAGES - 1) as i:
                body(i, True, True, True)
            body(IMAGES - 1, True, True, False)
            body(IMAGES, False, True, False)

        @block.sync
        def _(sp):
            def wait(s, v):
                sp.wait_ge(s, v)
                sp.nop(nofuse=True)

            def load_x(j):
                for g in range(G):
                    lo, hi = max(0, QR * g - 1), min(H, QR * g + QR + 1)
                    at0 = lo - (QR * g - 1)
                    sp.dma_start(xraw[C * g:C * g + C, at0:at0 + hi - lo, :], x[j, :, lo:hi, :]).then_inc(x_in, 16)

            def keep_x(j):
                sp.dma_start(xkeep[:, :], xraw[:, 1:QR + 1, :].rearrange("p r w -> p (r w)")).then_inc(x_kept, 16)

            def store(j):
                wait(out_done, at(j, 2, 2))
                for s in range(4):
                    dst = out[j, :, :, :].rearrange("c (q s) w -> c q s w", s=4)[:, :, s, :]
                    sp.dma_start(dst, x2r[C * s:C * s + C, :, :]).then_inc(out_st, 16)

            def by_slots(i):
                wait(x2_part, at(i, 4, 4))
                if sure(i):
                    wait(xq_lo_done, at(i, 4, 0))
                for g in range(G):
                    for s in range(4):
                        first = (2, 1, 1, 0)[s] + QR // 2 * g
                        sp.dma_start(x2q[C * s:C * s + C, first:first + QR // 2, :],
                                     x2[C * g:C * g + C, (s + 1) % 2, :, :]).then_inc(x2q_in, 16)

            def by_quads(i):
                wait(x2s_done, at(i, 1, 1))
                if sure(i):
                    wait(out_st, at(i, 64, 0))
                for g in range(G):
                    for s in range(4):
                        sp.dma_start(x2r[C * s:C * s + C, 4 * g:4 * g + 4, :],
                                     x2s[C * g:C * g + C, s, :, :]).then_inc(x2r_in, 16)

            def body(i, back, conv, front):
                if front:
                    wait(xn_done, at(i, 2, 2))
                    wait(x_kept, at(i, 16, 16))
                    load_x(i + 1)
                if sure(i, 2):
                    store(i - 2)
                if sure(i):
                    by_quads(i - 1)
                if back:
                    by_slots(i)
                if front:
                    wait(x_in, at(i + 1, 64, 64))
                    keep_x(i + 1)

            for n, (dst, src) in enumerate([
                    (geo_w_sb, geo_w), (geo_bias_sb, geo_bias), (val_w_sb, val_w), (pw_t_sb, pw_t),
                    (pw_b_sb, pw_b), (ident_sb, ident), (sel1_sb, sel_quarter),
                    (masks_sb, masks), (consts_sb, consts)]):
                if n == 0:
                    load_x(0)
                sp.dma_start(dst[:, :], src).then_inc(consts_in, 16)
            wflat = prod[:, 0:2, :].rearrange("p n f -> p (n f)")
            for dst0, src, n in ((0, w1, 3), (3, w2, 6), (9, w3, 9)):
                sp.dma_start(wflat[:, dst0 * P:(dst0 + n) * P], src).then_inc(consts_in, 16)
            wait(x_in, 64)
            keep_x(0)
            run_images(sp, body)
            store(IMAGES - 1)
            wait(out_st, 16 * 4 * IMAGES)

        ALL_CONST = 16 * (NCONST + 3)

        def conv_terms(n):
            layer, j0, m = CHUNKS[n]
            if layer == 1:
                for dx in range(3):
                    yield dx, xq_hi[:, j0:j0 + m, dx:dx + W], xq_lo[:, j0:j0 + m, dx:dx + W]
            if layer == 2:
                for t in range(2):
                    for dx in range(3):
                        yield (3 + 3 * t + dx, c1_hi[:, j0 + t:j0 + t + m, dx:dx + W],
                               c1_lo[:, j0 + t:j0 + t + m, dx:dx + W])
            if layer == 3:
                for t in range(3):
                    a, b = 2 * j0 + t, 2 * (j0 + m - 1) + t + 1
                    for dx in range(3):
                        yield 9 + 3 * t + dx, c2_hi[:, a:b:2, dx:dx + W], c2_lo[:, a:b:2, dx:dx + W]

        def conv_cols(n):
            return CHUNKS[n][2] * W

        def lo_needed(n):
            layer, j0, m = CHUNKS[n]
            if layer == 2:
                return min(4, (j0 + m - 1) // 8 + 1)
            return 9 if n == 10 else 4 + 3

        @block.tensor
        def _(pe):
            def conv_steps(j):
                for n in range(len(CHUNKS)):
                    if n == 0:
                        if sure(j):
                            pe.wait_ge(out_done, at(j, 2, 0))
                    elif 2 <= n < N_SPLIT + 2 and n - 2 < N_SPLIT:
                        pe.wait_ge(lo_done, at(j, N_SPLIT, n - 1))
                    if n < 4:
                        pe.wait_ge(xq_lo_done, at(j, 4, n + 1))
                    else:
                        pe.wait_ge(lo_done, at(j, N_SPLIT, lo_needed(n)))
                    terms = list(conv_terms(n))
                    dst = conv_ps[n % 2][:, 0:conv_cols(n)]
                    for m, (w, hi, lo) in enumerate(terms):
                        w_h, w_l = wc_hi[:, w * P:(w + 1) * P], wc_lo[:, w * P:(w + 1) * P]
                        last = m == len(terms) - 1
                        nc.tensor.matmul(dst, w_h, hi, start=m == 0, stop=False)
                        yield
                        nc.tensor.matmul(dst, w_h, lo, start=False, stop=False)
                        yield
                        mm = nc.tensor.matmul(dst, w_l, hi, start=False, stop=last)
                        if last:
                            mm.then_inc(conv_done, 1)
                        yield

            def values(i, u):
                if u >= 2 or sure(i):
                    pe.wait_ge(mult_done, at(i, UNITS, u - 1))
                h, tap = u // TAPS, UNIT_TAP[u % TAPS]
                if u == 0:
                    pe.wait_ge(pairs_done, at(i, 4, 4))
                for kk in range(K8 // 2):
                    k = h * K8 // 2 + kk
                    src = tap_x[:, tap, 2 * k:2 * k + 2, :].rearrange("p r w -> p (r w)")
                    mm = nc.tensor.matmul(val_ps[u % 2][:, kk * P:(kk + 1) * P], src, val_w_sb[:, :],
                                          start=kk == 0, stop=kk == K8 // 2 - 1, skip_group_check=True)
                mm.then_inc(val_done, 1)

            def transpose_sums(i, n):
                h, g = n // 4, n % 4
                if g == 0:
                    pe.wait_ge(mult_done, at(i, UNITS, 5 * h + 5))
                    pe.wait_ge(add_done, at(i, 2 * ADDS, ADDS * h + ADDS))
                if n >= 2 or sure(i):
                    pe.wait_ge(agg_sb, at(i, 8, n - 1))
                bufs = [PROD_BUF[5 * h + q] for q in (4, 0)]
                for kk in range(K8 // 2):
                    at0 = (kk * G + g) * P
                    for m, b in enumerate(bufs):
                        mm = nc.tensor.matmul(agg_ps[n % 2][:, kk * P:(kk + 1) * P], prod[:, b, at0:at0 + P],
                                              ident_sb[:, :], is_transpose=True, start=m == 0,
                                              stop=m == len(bufs) - 1)
                mm.then_inc(agg_t, 1)

            def pointwise(i, n):
                h, g = n // 4, n % 4
                if n == 0 and sure(i):
                    pe.wait_ge(gn2_v, at(i, GN_V, 0))
                if g == 0 and (h or sure(i)):
                    pe.wait_ge(x2_part, at(i, 4, 2 * h))
                pe.wait_ge(agg_sb, at(i, 8, n + 1))
                mm = nc.tensor.matmul(pw_ps[C * g:C * g + C, :], pw_t_sb[:, :], agg[:, n % 2, :],
                                      start=True, stop=True)
                mm.then_inc(pw_each, 1)

            def gn_sum(sem_v, value, sel, src, dst, done):
                pe.wait_ge(sem_v, value)
                nc.tensor.matmul(dst, sel[:, :], src, start=True, stop=True).then_inc(done, 1)

            def geometry(i):
                pe.wait_ge(xn_done, at(i, 2, 1))
                for k in range(K8):
                    mm = nc.tensor.matmul(geo_ps[:, k * GEO:(k + 1) * GEO],
                                          tap_x[:, 0, 2 * k:2 * k + 2, :].rearrange("p r w -> p (r w)"),
                                          geo_w_sb[:, :],
                                          start=k == 0, stop=k == K8 - 1, skip_group_check=True)
                mm.then_inc(geo_done, 1)

            def gn1_sums(i, n):
                if n == 0:
                    if sure(i):
                        pe.wait_ge(ch_v, at(i - 1, CH_V, 1))
                    gn_sum(gn1_v, at(i, GN_V, 3), sel1_sb, mv1[:, 0:1], geo_ps[:, 0:1], gn1_pe)
                else:
                    gn_sum(gn1_v, at(i, GN_V, 6), sel1_sb, gn1[:, 2:3], geo_ps[:, 1:2], gn1_pe)

            def gn2_sums(i, n):
                if n == 0:
                    pe.wait_ge(x2_part, at(i, 4, 4))
                    gn_sum(gn2_v, at(i, GN_V, 3), sel1_sb, mv2[:, 0:1], pw_ps[:, 0:1], gn2_pe)
                else:
                    gn_sum(gn2_v, at(i, GN_V, 6), sel1_sb, gn2[:, 2:3], pw_ps[:, 1:2], gn2_pe)

            def body(i, back, conv, front):
                steps = conv_steps(i - 1) if conv else iter(())

                def convs(n):
                    for _ in range(n):
                        next(steps, None)

                if back:
                    for u in range(UNITS):
                        values(i, u)
                        convs((4, 5, 5, 5, 5, 5, 5, 5, 1, 2)[u])
                        if front and u == 4:
                            gn1_sums(i + 1, 0)
                        if front and u == 6:
                            gn1_sums(i + 1, 1)
                        if u == 8:
                            transpose_sums(i, 0)
                            transpose_sums(i, 1)
                            convs(2)
                            for n in (0, 1):
                                transpose_sums(i, n + 2)
                                pointwise(i, n)
                            pointwise(i, 2)
                        if u == 9:
                            pointwise(i, 3)
                if front:
                    convs(3)
                    geometry(i + 1)
                if back:
                    convs(27)
                    transpose_sums(i, 4)
                    transpose_sums(i, 5)
                    convs(4)
                    for n in (4, 5):
                        transpose_sums(i, n + 2)
                        pointwise(i, n)
                    convs(4)
                    pointwise(i, 6)
                    pointwise(i, 7)
                    convs(16)
                    gn2_sums(i, 0)
                    convs(6)
                    gn2_sums(i, 1)
                for _ in steps:
                    pass

            pe.wait_ge(consts_in, ALL_CONST)
            gn1_sums(0, 0)
            gn1_sums(0, 1)
            pe.wait_ge(pads, N_PADS)
            pe.wait_ge(edges, N_EDGES)
            geometry(0)
            pe.wait_ge(w_lo, 1)
            run_images(pe, body)

        @block.vector
        def _(dve):
            v = nc.vector

            def lo_region(n):
                layer, j0, m = CHUNKS[n]
                ps = conv_ps[n % 2][:, 0:conv_cols(n)].rearrange("p (j w) -> p j w", w=W)
                if layer == 1:
                    sl = slice(1 + j0, 1 + j0 + m)
                    return [(ps, c1_hi[:, sl, 1:1 + W], c1_lo[:, sl, 1:1 + W])]
                half = [(0, P, 0, m)]
                if j0 == 0:
                    half = [(MID, P, 0, 1), (0, P, 1, m)]
                if j0 + m == H // 2 + 1:
                    half = [(0, MID, m - 1, m), (0, P, 0, m - 1)]
                return [(ps[a:b, s:e], c2_hi[a:b, j0 + s:j0 + e, 1:1 + W], c2_lo[a:b, j0 + s:j0 + e, 1:1 + W])
                        for a, b, s, e in half]

            def low_part(j, n):
                dve.wait_ge(hi_done, at(j, N_SPLIT, n + 1))
                for ps, hi, lo in lo_region(n):
                    op = v.tensor_tensor(lo, ps, hi.bitcast(F32), ALU.subtract)
                op.then_inc(lo_done, 1)

            def result(j, n):
                dve.wait_ge(conv_done, at(j, len(CHUNKS), N_SPLIT + n + 1))
                if n == 0:
                    dve.wait_ge(x2r_in, at(j, 256, 256))
                ps = conv_ps[(N_SPLIT + n) % 2][:, :].rearrange("p (j w) -> p j w", w=W)
                v.tensor_tensor(x2r[:, 8 * n:8 * n + 8, :], ps, x2r[:, 8 * n:8 * n + 8, :],
                                ALU.add).then_inc(out_done, 1)

            def mult(i, u):
                h, tap = u // TAPS, UNIT_TAP[u % TAPS]
                dve.wait_ge(val_done, at(i, UNITS, u + 1))
                if u == 0:
                    dve.wait_ge(ch_v, at(i, CH_V, 29))
                    if sure(i):
                        dve.wait_ge(agg_t, at(i, 8, 0))
                if u >= 7:
                    dve.wait_ge(add_done, at(i, 2 * ADDS, u - 6))
                B = K8 // 2 * G
                val = val_ps[u % 2][:, :].rearrange("p (b c) -> p b c", c=C)
                wgt = tapw[:, tap, h * B * R:(h + 1) * B * R].rearrange("p (b r) -> p b r", r=R)
                dst = prod[:, PROD_BUF[u], :].rearrange("p (b r c) -> p b r c", r=R, c=C)
                v.tensor_tensor(dst, val.unsqueeze(2).to_broadcast([P, B, R, C]),
                                wgt.unsqueeze(3).to_broadcast([P, B, R, C]), ALU.mult).then_inc(mult_done, 1)

            def residual(i, h):
                dve.wait_ge(pw_each, at(i, 8, 4 * h + 4))
                if h == 0:
                    dve.wait_ge(x_kept, at(i, 16, 16))
                    if sure(i):
                        dve.wait_ge(x2q_in, at(i, 256, 0))
                        dve.wait_ge(x2s_done, at(i, 1, 0))
                def rows(t, parity):
                    return t.rearrange("p (k t w) -> p t k w", t=2, w=W)[:, parity]
                kept = xkeep[:, h * BANK:(h + 1) * BANK]
                half = x2[:, :, 4 * h:4 * h + 4, :]
                for parity in range(2):
                    op = v.scalar_tensor_tensor(half[:, parity], rows(pw_ps[:, :], parity), pw_b_sb[:, 0:1],
                                                rows(kept, parity), ALU.add, ALU.add)
                    op.then_inc(x2_part, 1)
                dve.wait_ge(x2_part, at(i, 4, 2 * h + 2))
                v.bn_stats(st2[:, h, :], half).then_inc(gn2_v, 1)

            def aggregate(i, st, mv, sv):
                dve.wait_ge(sv, at(i, GN_V, 2))
                dve.nop(nofuse=True)
                v.bn_aggr(mv[:, :], st[:, :, :].rearrange("p a b -> p (a b)")).then_inc(sv, 1)

            def gn_spread(i, sv, mv, t, ps, pe_sem):
                dve.wait_ge(pe_sem, at(i, 2, 1))
                v.tensor_copy(t[:, 0:1], ps[:, 0:1]).then_inc(sv, 1)
                v.tensor_tensor(t[:, 1:2], mv[:, 0:1], ps[:, 0:1], ALU.subtract).then_inc(sv, 1)
                dve.wait_ge(sv, at(i, GN_V, 5))
                v.scalar_tensor_tensor(t[:, 2:3], t[:, 1:2], t[:, 1:2], mv[:, 1:2],
                                       ALU.mult, ALU.add).then_inc(sv, 1)

            def gn_eps(i, sv, t, ps, pe_sem):
                dve.wait_ge(pe_sem, at(i, 2, 2))
                v.tensor_scalar(t[:, 3:4], ps[:, 1:2], EPS_GN, None, ALU.add).then_inc(sv, 1)

            def gn_scale(i, sv, t, pow_sem):
                dve.wait_ge(pow_sem, at(i, 1, 1))
                v.tensor_scalar(t[:, 6:9], masks_sb[:, :], t[:, 4:5], None, ALU.mult)\
                    .then_inc(sv, 1)
                dve.wait_ge(sv, at(i, GN_V, 8))
                v.tensor_scalar(t[:, 9:12], t[:, 6:9], t[:, 0:1], -1.0, ALU.mult, ALU.mult).then_inc(sv, 1)

            def gn1_a(i):
                dve.wait_ge(x_in, at(i, 64, 64))
                for n in range(2):
                    v.bn_stats(st1[:, n, :], xraw[:, 1 + 8 * n:9 + 8 * n, :].rearrange("p r w -> p (r w)"))\
                        .then_inc(gn1_v, 1)
                aggregate(i, st1, mv1, gn1_v)

            def gn1_b(i):
                gn_spread(i, gn1_v, mv1, gn1, geo_ps, gn1_pe)

            def gn1_c(i):
                gn_eps(i, gn1_v, gn1, geo_ps, gn1_pe)

            def gn1_d(i):
                gn_scale(i, gn1_v, gn1, gn1_pow)

            def link(i, s, per, k, op):
                op.then_inc(s, 1)
                dve.wait_ge(s, at(i, per, k))

            def chain(i):
                gate, theta = geo[:, 0, :], geo[:, 1, :]
                raw = geo[:, 2:4, :]
                e, gs = ch[:, 0, :], ch[:, 1, :]
                th, kk, th2 = ch[:, 2, :], ch[:, 3, :], ch[:, 4, :]
                lb = ch[:, 14, :]
                t, w = ch[:, 6:8, :], ch[:, 8:10, :]
                l, spl = ch[:, 10:12, :], ch[:, 12:14, :]

                def step(k, op):
                    link(i, ch_v, CH_V, k, op)

                def need_act(k):
                    dve.wait_ge(ch_a, at(i, CH_A, k))

                dve.wait_ge(geo_done, at(i, 1, 1))
                src = geo_ps[:, :].rearrange("p (k q j) -> p q k j", q=4, j=G * R)
                bias = geo_bias_sb[:, :].rearrange("p (q j) -> p q j", q=4).unsqueeze(2)\
                    .to_broadcast([P, 4, K8, G * R])
                step(1, v.tensor_tensor(geo[:, :, :].rearrange("p q (k j) -> p q k j", j=G * R), src, bias, ALU.add))
                step(2, v.tensor_scalar(kk, theta, INV_2PI, ROUND, ALU.mult, ALU.add))
                step(3, v.tensor_scalar(kk, kk, -ROUND, None, ALU.add))
                step(4, v.scalar_tensor_tensor(th, kk, -TWO_PI_HI, theta, ALU.mult, ALU.add))
                step(5, v.scalar_tensor_tensor(th, kk, -TWO_PI_LO, th, ALU.mult, ALU.add))
                step(6, v.tensor_scalar(th2, th, PI_BELOW, -PI_BELOW, ALU.min, ALU.max))
                g4 = gate.rearrange("p (b r) -> p b r", r=R)
                step(7, v.tensor_reduce(small[:, 0, :], g4, AX.X, ALU.max))
                step(8, v.tensor_tensor(gs.rearrange("p (b r) -> p b r", r=R), g4,
                                        small[:, 0, :].unsqueeze(2).to_broadcast([P, K8 * G, R]), ALU.subtract))
                need_act(2)
                step(9, v.tensor_scalar(w, t, 1.0, None, ALU.add))
                step(10, v.scalar_tensor_tensor(t, w, -1.0, t, ALU.add, ALU.subtract))
                yield
                need_act(4)
                step(11, v.tensor_tensor(l, l, t, ALU.subtract))
                step(12, v.scalar_tensor_tensor(spl, raw, 0.0, l, ALU.max, ALU.add))
                yield
                need_act(5)
                step(13, v.tensor_tensor(w[:, 0, :], spl[:, 1, :], lb, ALU.add))
                step(14, v.tensor_tensor(w[:, 1, :], spl[:, 1, :], lb, ALU.subtract))
                yield
                need_act(10)
                step(15, v.tensor_tensor(trig[:, 2, :], trig[:, 0, :], trig[:, 1, :], ALU.add))
                step(16, v.tensor_tensor(trig[:, 3, :], trig[:, 0, :], trig[:, 1, :], ALU.subtract))
                yield
                need_act(11)
                sq = trig2[:, :, :]
                step(17, v.tensor_tensor(expo[:, :], sq, t[:, 0, :].unsqueeze(1).to_broadcast([P, 4, NW]), ALU.mult))
                step(18, v.tensor_tensor(sq, sq, t[:, 1, :].unsqueeze(1).to_broadcast([P, 4, NW]), ALU.mult))
                ea = expo[:, :].rearrange("p (h w) n -> p h w n", w=2)
                eb = sq.rearrange("p (h w) n -> p h w n", w=2)
                step(19, v.tensor_tensor(ea[:, :, 0], ea[:, :, 0], eb[:, :, 1], ALU.add))
                step(20, v.tensor_tensor(ea[:, :, 1], ea[:, :, 1], eb[:, :, 0], ALU.add))
                yield
                need_act(12)
                kern = trig[:, :, :]
                step(21, v.tensor_reduce(kk, kern.rearrange("p t n -> p n t"), AX.X, ALU.add))
                step(22, v.tensor_scalar(kk, kk, 2.0, 1.0, ALU.mult, ALU.add))
                step(23, v.tensor_tensor(kk, kk, e, ALU.mult))
                step(24, v.tensor_reduce(small[:, 1, :], kk.rearrange("p (b r) -> p b r", r=R), AX.X, ALU.add))
                step(25, v.tensor_reduce(small[:, 2, :], e.rearrange("p (b r) -> p b r", r=R), AX.X, ALU.add))
                step(26, v.scalar_tensor_tensor(small[:, 3, :], small[:, 2, :], EPS_Z, small[:, 1, :],
                                                ALU.mult, ALU.add))
                step(27, v.reciprocal(small[:, 4, :], small[:, 3, :]))
                step(28, v.tensor_tensor(tapw[:, 0, :].rearrange("p (b r) -> p b r", r=R),
                                         e.rearrange("p (b r) -> p b r", r=R),
                                         small[:, 4, :].unsqueeze(2).to_broadcast([P, K8 * G, R]), ALU.mult))
                step(29, v.tensor_tensor(tapw[:, 1:TAPS, :], kern,
                                         tapw[:, 0, :].unsqueeze(1).to_broadcast([P, 4, NW]), ALU.mult))
                yield

            def split_low(i, n):
                dve.wait_ge(xq_act, at(i, 8, 2 * n + 2))
                rows = slice(8 * n, 8 * n + 8)
                v.tensor_tensor(xq_lo[:, rows, 1:1 + W], x2q[:, 8 * n + 1:8 * n + 9, :],
                                xq_hi[:, rows, 1:1 + W].bitcast(F32), ALU.subtract).then_inc(xq_lo_done, 1)

            def body(i, back, conv, front):
                j = i - 1
                weights = chain(i + 1) if front else iter(())

                def low(n):
                    if conv:
                        low_part(j, n)

                def part():
                    next(weights, None)

                if back:
                    for u in range(UNITS):
                        mult(i, u)
                        if u in (2, 4, 6, 8):
                            low(u // 2 - 1)
                        if front and u == 2:
                            gn1_a(i + 1)
                        if front and u == 5:
                            gn1_b(i + 1)
                        if front and u == 6:
                            gn1_c(i + 1)
                        if front and u == 8:
                            gn1_d(i + 1)
                    residual(i, 0)
                else:
                    for n in range(4):
                        low(n)
                part()
                low(4)
                part()
                low(5)
                if back:
                    residual(i, 1)
                    aggregate(i, st2, mv2, gn2_v)
                part()
                if back:
                    gn_spread(i, gn2_v, mv2, gn2, pw_ps, gn2_pe)
                part()
                low(6)
                if back:
                    gn_eps(i, gn2_v, gn2, pw_ps, gn2_pe)
                part()
                low(7)
                if back:
                    gn_scale(i, gn2_v, gn2, gn2_pow)
                part()
                low(8)
                part()
                if conv:
                    result(j, 0)
                if back:
                    for n in range(4):
                        split_low(i, n)
                if conv:
                    result(j, 1)

            for rows in (xraw[0:C, 0, :], xraw[3 * C:P, QR + 1, :], x2q[0:C, 1, :], x2q[3 * C:P, H // 2, :]):
                v.memset(rows, 0.0).then_inc(edges, 1)
            for tile in (c2_hi, c2_lo):
                v.memset(tile[0:MID, 0, 1:1 + W].bitcast(F32), 0.0).then_inc(edges, 1)
                v.memset(tile[MID:P, H // 2, 1:1 + W].bitcast(F32), 0.0).then_inc(edges, 1)
            dve.wait_ge(consts_in, ALL_CONST)
            gn1_a(0)
            gn1_b(0)
            gn1_c(0)
            gn1_d(0)
            dve.wait_ge(w_hi, 1)
            v.tensor_tensor(wc_lo[:, :], prod[:, 0:2, :].rearrange("p n f -> p (n f)")[:, 0:NC],
                            wc_hi[:, :].bitcast(F32), ALU.subtract).then_inc(w_lo, 1)
            dve.wait_ge(w_lo, 1)
            for _ in chain(0):
                pass
            run_images(dve, body)

        @block.scalar
        def _(act):
            s = nc.scalar
            C_PI2, C_EPSB, C_MH, C_PH, C_ONE = (consts_sb[:, k:k + 1] for k in range(5))

            def hi_part(j, n):
                act.wait_ge(conv_done, at(j, len(CHUNKS), n + 1))
                layer, j0, m = CHUNKS[n]
                ps = conv_ps[n % 2][:, 0:conv_cols(n)].rearrange("p (j w) -> p j w", w=W)
                if layer == 1:
                    parts = [(ps, c1_hi[:, 1 + j0:1 + j0 + m, 1:1 + W])]
                else:
                    half = [(0, P, 0, m)]
                    if j0 == 0:
                        half = [(MID, P, 0, 1), (0, P, 1, m)]
                    if j0 + m == H // 2 + 1:
                        half = [(0, MID, m - 1, m), (0, P, 0, m - 1)]
                    parts = [(ps[a:b, q:r], c2_hi[a:b, j0 + q:j0 + r, 1:1 + W]) for a, b, q, r in half]
                for src, dst in parts:
                    op = s.activation(dst, src, ACT.Copy)
                op.then_inc(hi_done, 1)

            def sums_out(i, n):
                act.wait_ge(agg_t, at(i, 8, n + 1))
                if n >= 2 or sure(i):
                    act.wait_ge(pw_each, at(i, 8, n - 1))
                s.activation(agg[:, n % 2, :], agg_ps[n % 2][:, :], ACT.Copy).then_inc(agg_sb, 1)

            def norm1(i):
                act.wait_ge(gn1_v, at(i, GN_V, GN_V))
                if sure(i):
                    act.wait_ge(val_done, at(i, UNITS, 0))
                    act.wait_ge(pairs_done, at(i, 4, 0))
                s.activation(tap_x[:, 0], xraw[:, 1:QR + 1, :], ACT.Identity,
                             scale=gn1[:, 6:7], bias=gn1[:, 9:10]).then_inc(xn_done, 1)
                for row, n, m in ((0, 1, 1), (QR + 1, 1, 2), (1, QR, 0)):
                    op = s.activation(xn[:, row:row + n, 1:1 + W], xraw[:, row:row + n, :], ACT.Identity,
                                      scale=gn1[:, 6 + m:7 + m], bias=gn1[:, 9 + m:10 + m])
                op.then_inc(xn_done, 1)

            def chain(i):
                gs = ch[:, 1, :]
                th2, tha = ch[:, 4, :], ch[:, 5, :]
                t, w, l, spl = ch[:, 6:8, :], ch[:, 8:10, :], ch[:, 10:12, :], ch[:, 12:14, :]
                lb = ch[:, 14, :]

                def need(k):
                    act.wait_ge(ch_v, at(i, CH_V, k))

                def step(k, op):
                    op.then_inc(ch_a, 1)
                    act.wait_ge(ch_a, at(i, CH_A, k))

                need(1)
                step(1, s.activation(t, geo[:, 2:4, :], ACT.Abs))
                step(2, s.activation(t, t, ACT.Exp, scale=-1.0))
                need(8)
                step(3, s.activation(ch[:, 0, :], gs, ACT.Exp))
                need(10)
                step(4, s.activation(l, w, ACT.Ln))
                yield
                need(12)
                step(5, s.activation(lb, spl[:, 0, :], ACT.Ln, bias=C_EPSB))
                need(14)
                step(6, s.activation(t[:, 0, :], w[:, 0, :], ACT.Exp, scale=-2.0, bias=C_MH))
                step(7, s.activation(t[:, 1, :], w[:, 1, :], ACT.Exp, scale=2.0, bias=C_PH))
                step(8, s.activation(tha, th2, ACT.Abs))
                step(9, s.activation(trig[:, 1, :], th2, ACT.Sin))
                step(10, s.activation(trig[:, 0, :], tha, ACT.Sin, scale=-1.0, bias=C_PI2))
                act.nop(nofuse=True)
                s.preload_act_table_set(EXP_SET)
                yield
                need(16)
                step(11, s.activation(trig2[:, :, :], trig[:, :, :], ACT.Square))
                need(20)
                step(12, s.activation(trig[:, :, :], expo[:, :], ACT.Exp, scale=-1.0))
                yield

            def split_high(i, n):
                if n == 0:
                    act.wait_ge(gn2_v, at(i, GN_V, GN_V))
                    act.wait_ge(x2q_in, at(i, 256, 256))
                    if sure(i):
                        act.wait_ge(conv_done, at(i - 1, len(CHUNKS), 4))
                parts = [(8 * n, 8 * n + 8, 0)]
                if n == 0:
                    parts = [(0, 1, 1), (1, 8, 0)]
                if n == 3:
                    parts = [(H // 2 - 1, H // 2, 2), (24, H // 2 - 1, 0)]
                for a, b, m in parts:
                    op = s.activation(x2q[:, a + 1:b + 1, :], x2q[:, a + 1:b + 1, :], ACT.Identity,
                                      scale=gn2[:, 6 + m:7 + m], bias=gn2[:, 9 + m:10 + m])
                op.then_inc(xq_act, 1)
                act.wait_ge(xq_act, at(i, 8, 2 * n + 1))
                s.activation(xq_hi[:, 8 * n:8 * n + 8, 1:1 + W], x2q[:, 8 * n + 1:8 * n + 9, :],
                             ACT.Copy).then_inc(xq_act, 1)

            def quad_rows(i):
                act.wait_ge(x2_part, at(i, 4, 4))
                if sure(i):
                    act.wait_ge(x2r_in, at(i, 256, 0))
                for parity in range(2):
                    dst = x2s[:, parity::2, :, :]
                    src = x2[:, parity, :, :].rearrange("p (q a) w -> p a q w", a=2)
                    op = s.activation(dst, src, ACT.Copy)
                op.then_inc(x2s_done, 1)

            def body(i, back, conv, front):
                j = i - 1
                weights = chain(i + 1) if front else iter(())

                def high(n):
                    if conv:
                        hi_part(j, n)

                for n in range(4):
                    high(n)
                if back:
                    for n in range(4):
                        sums_out(i, n)
                if front:
                    norm1(i + 1)
                next(weights, None)
                high(4)
                if back:
                    for n in range(4, 8):
                        sums_out(i, n)
                high(5)
                next(weights, None)
                if back:
                    quad_rows(i)
                high(6)
                next(weights, None)
                high(7)
                high(8)
                if back:
                    for n in range(4):
                        split_high(i, n)

            s.preload_act_table_set(EXP_SET)
            act.wait_ge(consts_in, ALL_CONST)
            s.activation(wc_hi[:, :], prod[:, 0:2, :].rearrange("p n f -> p (n f)")[:, 0:NC], ACT.Copy)\
                .then_inc(w_hi, 1)
            act.wait_ge(edges, N_EDGES)
            norm1(0)
            for _ in chain(0):
                pass
            run_images(act, body)

        @block.gpsimd
        def _(pool):
            p = nc.gpsimd

            def rstd(i, t, sv, done):
                pool.wait_ge(sv, at(i, GN_V, 7))
                p.tensor_tensor(t[:, 4:5], t[:, 3:4], t[:, 5:6], ALU.pow).then_inc(done, 1)

            def add_pair(i, n):
                h, m = n // ADDS, n % ADDS
                u = 5 * h + (0, 2, 0)[m]
                if m < 2:
                    pool.wait_ge(mult_done, at(i, UNITS, u + 2))
                else:
                    pool.wait_ge(add_done, at(i, 2 * ADDS, n))
                a, b = PROD_BUF[u], PROD_BUF[u + (1, 1, 2)[m]]
                p.tensor_tensor(prod[:, a, :], prod[:, a, :], prod[:, b, :], ALU.add).then_inc(add_done, 1)

            def shifted_sum(i, n):
                up, mid, down = slice(0, QR), slice(1, QR + 1), slice(2, QR + 2)
                left, here, right = slice(0, W), slice(1, 1 + W), slice(2, 2 + W)
                a, b = (((mid, left), (mid, right)), ((up, here), (down, here)),
                        ((up, left), (down, right)), ((up, right), (down, left)))[n]
                if n == 0:
                    pool.wait_ge(xn_done, at(i, 2, 2))
                p.tensor_tensor(tap_x[:, 1 + n], xn[:, a[0], a[1]], xn[:, b[0], b[1]],
                                ALU.add).then_inc(pairs_done, 1)

            def body(i, back, conv, front):
                if back:
                    for n in range(3):
                        add_pair(i, n)
                    if front:
                        rstd(i + 1, gn1, gn1_v, gn1_pow)
                    for n in range(3, 6):
                        add_pair(i, n)
                if front:
                    pool.wait_ge(val_done, at(i, UNITS, UNITS))
                    shifted_sum(i + 1, 0)
                    shifted_sum(i + 1, 1)
                if back:
                    rstd(i, gn2, gn2_v, gn2_pow)
                if front:
                    shifted_sum(i + 1, 2)
                    shifted_sum(i + 1, 3)

            for tile in (xn, xq_hi, xq_lo, c1_hi, c1_lo, c2_hi, c2_lo):
                for col in (0, PW - 1):
                    p.memset(tile[:, :, col:col + 1].bitcast(F32), 0.0).then_inc(pads, 1)
            for tile in (c1_hi, c1_lo):
                for row in (0, H // 2 + 1):
                    p.memset(tile[:, row, 1:1 + W].bitcast(F32), 0.0).then_inc(pads, 1)
            p.memset(gn1[:, 5:6], -0.5).then_inc(pads, 1)
            p.memset(gn2[:, 5:6], -0.5).then_inc(pads, 1)
            pool.wait_ge(pads, N_PADS)
            rstd(0, gn1, gn1_v, gn1_pow)
            for n in range(4):
                shifted_sum(0, n)
            run_images(pool, body)


def kernel(**inputs):
    import numpy as np
    import concourse.bacc as bacc
    from concourse import mybir as mb
    from concourse.bass_utils import run_bass_kernel_spmd

    a = {k: np.asarray(v) for k, v in inputs.items()}
    f = np.float32
    rows = np.concatenate([a["L0_conv_gate_w"], a["L0_conv_geom_w"]], axis=0).reshape(4, R, C)
    bias = np.concatenate([a["L0_conv_gate_b"], a["L0_conv_geom_b"]], axis=0).reshape(4, R)
    geo_w = np.zeros((G, C, 4, G, R), f)
    geo_bias = np.zeros((P, 4, G, R), f)
    val_w = np.zeros((G, C, G, C), f)
    for g in range(G):
        geo_w[g, :, :, g, :] = rows.transpose(2, 0, 1)
        geo_bias[:, :, g, :] = bias
        val_w[g, :, g, :] = a["L0_conv_value_w"].T
    pw_b = np.zeros((G, C, 1), f)
    pw_b[:, :, 0] = a["L0_conv_pw_b"]

    def banded(w, rows_in, rows_out, groups, step):
        o, c = w.shape[:2]
        m = np.zeros((rows_in, c, groups, 3, rows_out, o), f)
        for t in range(groups):
            for ri in range(rows_in):
                for ro in range(rows_out):
                    ky = step * t + ri - ro
                    if 0 <= ky <= 2:
                        m[ri, :, t, :, ro, :] = w[:, :, ky, :].transpose(1, 2, 0)
        return m.reshape(rows_in * c, groups * 3 * rows_out * o)

    sel_quarter = np.zeros((G, C, G, C), f)
    for c in range(C):
        sel_quarter[:, c, :, c] = 1.0 / G
    masks = np.ones((P, 3), f)
    masks[0:C, 1] = 0.0
    masks[P - C:P, 2] = 0.0
    consts = np.zeros((P, 5), f)
    consts[:, :] = np.array([1.5707963267948966, EPS_BASE, -2 * MIN_HYP, 2 * MIN_HYP, 1.0], f)
    arrays = {
        "x": np.ascontiguousarray(a["x"]), "geo_w": geo_w.reshape(P, GEO), "geo_bias": geo_bias.reshape(P, GEO),
        "val_w": val_w.reshape(P, P), "pw_t": np.ascontiguousarray(a["L0_conv_pw_w"].T), "pw_b": pw_b.reshape(P, 1),
        "w1": banded(a["L1_conv_w1"], 4, 2, 1, 0), "w2": banded(a["L1_conv_w2"], 2, 2, 2, 2),
        "w3": banded(a["L1_conv_w3"], 2, 4, 3, 2), "ident": np.eye(P, dtype=f),
        "sel_quarter": sel_quarter.reshape(P, P), 
        "masks": masks, "consts": consts,
    }
    nc = bacc.Bacc("TRN2", target_bir_lowering=False, num_devices=1)
    args = [nc.dram_tensor(f"in_{k}", v.shape, mb.dt.from_np(v.dtype), kind="ExternalInput").ap()
            for k, v in arrays.items()]
    out = nc.dram_tensor("out_y", (IMAGES, C, H, W), F32, kind="ExternalOutput").ap()
    conv_l0_l1_kernel(nc, *args, out)
    r = run_bass_kernel_spmd(nc, [{f"in_{k}": v for k, v in arrays.items()}], core_ids=[0])
    return r.results[0]["out_y"]
```

```python
from collections import namedtuple
from contextlib import ExitStack

import concourse.bass as bass
from concourse import mybir

F32 = mybir.dt.float32
F32R = mybir.dt.float32r
ALU = mybir.AluOpType
ACT = mybir.ActivationFunctionType
AX = mybir.AxisListType

P = 128
IMAGES, C, H, W = 8, 32, 64, 64
G = 4
QR = H // G
K8 = QR // 2
R = 4
TAPS = 5
MID = 64
PW = W + 2
GEO = G * 4 * R
NW = K8 * G * R
UNITS = 2 * TAPS
HALF = K8 // 2 * G * P
BANK = 512

Norm = namedtuple("Norm", "st mv t ps v pe pow")

EXP_SET = "natural_log_exp_and_others"

EPS_GN = 1e-5
EPS_BASE = 1e-4
MIN_HYP = 0.1
EPS_Z = 1e-6
INV_2PI = 0.15915494309189535
TWO_PI_HI = 6.28125
TWO_PI_LO = 0.0019353071795864769
ROUND = 12582912.0
PI_BELOW = 3.1415925

UNIT_TAP = (1, 2, 3, 4, 0)
PROD_BUF = (0, 1, 2, 3, 4, 5, 1, 6, 3, 4)
N_PROD = 7

CHUNKS = ([(1, 8 * n, 8) for n in range(4)]
          + [(2, 0, 7), (2, 7, 7), (2, 14, 7), (2, 21, 6), (2, 27, 6)]
          + [(3, 0, 8), (3, 8, 8)])
TERMS = {1: 3, 2: 6, 3: 9}
CONV_PRODUCTS = [(n, term, part) for n, (layer, _, _) in enumerate(CHUNKS)
                 for term in range(TERMS[layer]) for part in range(3)]
N_SPLIT = 9
N_OUT = 2

GN_V = 9
ADDS = 4
DVE_SUMS = (1, 5, 7)
CH_V, CH_A = 29, 12


def conv_l0_l1_kernel(nc, x, geo_w, geo_bias, val_w, pw_t, pw_b, w1, w2, w3, ident, sel_quarter,
                      masks, consts, out):
    ctx = ExitStack()
    with ctx:
        def sb(name, shape, dt=F32):
            return ctx.enter_context(nc.sbuf_tensor(name, shape, dt))

        def pb(name):
            return ctx.enter_context(nc.psum_tensor(name, [P, BANK], F32))

        def sem(name):
            return ctx.enter_context(nc.semaphore(name))

        geo_w_sb = sb("geo_w_sb", [P, GEO])
        geo_bias_sb = sb("geo_bias_sb", [P, GEO])
        val_w_sb = sb("val_w_sb", [P, P])
        pw_t_sb = sb("pw_t_sb", [P, C])
        pw_b_sb = sb("pw_b_sb", [P, 1])
        ident_sb = sb("ident_sb", [P, P])
        sel1_sb = sb("sel1_sb", [P, P])
        masks_sb = sb("masks_sb", [P, 3])
        consts_sb = sb("consts_sb", [P, 4])
        NC = (3 + 6 + 9) * P
        wc_hi = sb("wc_hi", [P, NC], F32R)
        wc_lo = sb("wc_lo", [P, NC], F32R)
        xraw = sb("xraw", [P, QR + 2, W])
        xkeep = sb("xkeep", [P, QR * W])
        xn = sb("xn", [P, QR + 2, PW])
        xc = sb("xc", [P, QR, W])
        tap_x = sb("tap_x", [P, TAPS, QR, W])
        st1 = sb("st1", [P, 2, 6])
        mv1 = sb("mv1", [P, 2])
        gn1 = sb("gn1", [P, 16])
        geo = sb("geo", [P, 4, NW])
        ch = sb("ch", [P, 14, NW])
        trig = sb("trig", [P, 4, NW])
        trig2 = sb("trig2", [P, 4, NW])
        expo = sb("expo", [P, 4, NW])
        small = sb("small", [P, 5, K8 * G])
        tapw = sb("tapw", [P, TAPS, NW])
        prod = sb("prod", [P, N_PROD, HALF])
        w_stage = prod[:, 5:7, :].rearrange("p n f -> p (n f)")[:, 0:NC]
        agg = sb("agg", [P, 2, BANK])
        x2 = sb("x2", [P, 2, QR // 2, W])
        x2s = sb("x2s", [P, 4, QR // 4, W])
        x2q = sb("x2q", [P, H // 2 + 2, W])
        x2r = sb("x2r", [P, H // 4, W])
        st2 = sb("st2", [P, 2, 6])
        mv2 = sb("mv2", [P, 2])
        gn2 = sb("gn2", [P, 16])
        xq_hi = sb("xq_hi", [P, H // 2, PW], F32R)
        xq_lo = sb("xq_lo", [P, H // 2, PW], F32R)
        c1_hi = sb("c1_hi", [P, H // 2 + 2, PW], F32R)
        c1_lo = sb("c1_lo", [P, H // 2 + 2, PW], F32R)
        c2_hi = sb("c2_hi", [P, H // 2 + 1, PW], F32R)
        c2_lo = sb("c2_lo", [P, H // 2 + 1, PW], F32R)

        geo_ps = pb("geo_ps")
        val_ps = [pb("val_ps0"), pb("val_ps1")]
        agg_ps = [pb("agg_ps0"), pb("agg_ps1")]
        pw_ps = pb("pw_ps")
        conv_ps = [pb("conv_ps0"), pb("conv_ps1")]

        front_consts_in = sem("front_consts_in")
        back_consts_in = sem("back_consts_in")
        weights_in = sem("weights_in")
        w_high = sem("w_high")
        w_low = sem("w_low")
        pads = sem("pads")
        edges = sem("edges")
        x_in = sem("x_in")
        x_kept = sem("x_kept")
        gn1_v = sem("gn1_v")
        gn1_pe = sem("gn1_pe")
        gn1_pow = sem("gn1_pow")
        xn_done = sem("xn_done")
        centre_done = sem("centre_done")
        pairs_done = sem("pairs_done")
        geo_done = sem("geo_done")
        ch_v = sem("ch_v")
        ch_a = sem("ch_a")
        val_done = sem("val_done")
        mult_done = sem("mult_done")
        add_done = sem("add_done")
        dve_sum = sem("dve_sum")
        agg_t = sem("agg_t")
        agg_sb = sem("agg_sb")
        pw_pair = sem("pw_pair")
        x2_part = sem("x2_part")
        x2q_in = [sem(f"x2q_in_{g}") for g in range(G)]
        x2r_in = sem("x2r_in")
        gn2_v = sem("gn2_v")
        gn2_pe = sem("gn2_pe")
        gn2_pow = sem("gn2_pow")
        x2s_done = sem("x2s_done")
        xq_act = sem("xq_act")
        xq_lo_done = sem("xq_lo_done")
        conv_done = sem("conv_done")
        hi_done = sem("hi_done")
        lo_done = sem("lo_done")
        out_done = sem("out_done")
        out_st = sem("out_st")

        NORM1 = Norm(st1, mv1, gn1, geo_ps, gn1_v, gn1_pe, gn1_pow)
        NORM2 = Norm(st2, mv2, gn2, pw_ps, gn2_v, gn2_pe, gn2_pow)

        def at(i, per_image, n):
            return per_image * i + n

        def sure(i):
            return not isinstance(i, int) or i >= 1

        def on(i, step, *args):
            if not isinstance(i, int) or 0 <= i < IMAGES:
                step(i, *args)

        def ahead(i, step, *args):
            if not isinstance(i, int) or 1 <= i < IMAGES:
                step(i, *args)

        def sum_units(n):
            return [TAPS * (n // 4) + u for u in ((0, 1), (2, 3), (0, 2), (0, 4))[n % 4]]

        def sum_operands(n):
            return [prod[:, PROD_BUF[u], :] for u in sum_units(n)]

        block = ctx.enter_context(nc.Block())
        N_FRONT_CONSTS, N_BACK_CONSTS = 5, 4
        N_PADS = 7 * 2 + 2 * 2 + 2
        N_EDGES = 4 + 2 * 2

        def run_images(eng, body):
            body(0)
            body(1)
            with eng.Fori(2, IMAGES - 2) as i:
                body(i)
            for i in range(IMAGES - 2, IMAGES + 2):
                body(i)

        @block.sync
        def _(sp):
            def wait(s, v):
                sp.wait_ge(s, v)
                sp.nop(nofuse=True)

            def load_x(j):
                if sure(j):
                    wait(xn_done, at(j, 2, 0))
                for g in range(G):
                    lo, hi = max(0, QR * g - 1), min(H, QR * g + QR + 1)
                    at0 = lo - (QR * g - 1)
                    sp.dma_start(xraw[C * g:C * g + C, at0:at0 + hi - lo, :], x[j, :, lo:hi, :]).then_inc(x_in, 16)

            def keep_x(j):
                if sure(j):
                    wait(x2_part, at(j, 4, 0))
                for g in range(G):
                    sp.dma_start(xkeep[C * g:C * g + C, :],
                                 x[j, :, QR * g:QR * g + QR, :].rearrange("c r w -> c (r w)")).then_inc(x_kept, 16)

            def store(j):
                wait(out_done, at(j, 2, 2))
                for s in range(4):
                    dst = out[j, :, :, :].rearrange("c (q s) w -> c q s w", s=4)[:, :, s, :]
                    sp.dma_start(dst, x2r[C * s:C * s + C, :, :]).then_inc(out_st, 16)

            def by_slots(i, g):
                if g == 0:
                    wait(x2_part, at(i, 4, 4))
                    if sure(i):
                        wait(xq_lo_done, at(i, 4, 0))
                for s in range(4):
                    first = (2, 1, 1, 0)[s] + QR // 2 * g
                    sp.dma_start(x2q[C * s:C * s + C, first:first + QR // 2, :],
                                 x2[C * g:C * g + C, (s + 1) % 2, :, :]).then_inc(x2q_in[g], 16)

            def by_quads(i):
                wait(x2s_done, at(i, 1, 1))
                if sure(i):
                    wait(out_st, at(i, 64, 0))
                for g in range(G):
                    for s in range(4):
                        sp.dma_start(x2r[C * s:C * s + C, 4 * g:4 * g + 4, :],
                                     x2s[C * g:C * g + C, s, :, :]).then_inc(x2r_in, 16)

            def body(i):
                on(i - 1, by_slots, 0)
                on(i - 1, by_slots, 1)
                on(i - 1, by_slots, 2)
                on(i + 2, load_x)
                on(i - 1, by_slots, 3)
                on(i - 2, store)
                on(i - 1, by_quads)
                on(i, keep_x)

            load_x(0)
            for dst, src in ((sel1_sb, sel_quarter), (masks_sb, masks), (consts_sb, consts), (geo_w_sb, geo_w),
                             (geo_bias_sb, geo_bias)):
                sp.dma_start(dst[:, :], src).then_inc(front_consts_in, 16)
            for dst0, src, n in ((0, w1, 3), (3, w2, 6), (9, w3, 9)):
                sp.dma_start(w_stage[:, dst0 * P:(dst0 + n) * P], src).then_inc(weights_in, 16)
            for dst, src in ((val_w_sb, val_w), (ident_sb, ident), (pw_t_sb, pw_t), (pw_b_sb, pw_b)):
                sp.dma_start(dst[:, :], src).then_inc(back_consts_in, 16)
            load_x(1)
            run_images(sp, body)
            wait(out_st, 16 * 4 * IMAGES)

        def conv_operands(n, term):
            layer, j0, m = CHUNKS[n]
            t, dx = term // 3, term % 3
            cols = slice(dx, dx + W)
            if layer == 1:
                rows, hi, lo, first = slice(j0, j0 + m), xq_hi, xq_lo, 0
            elif layer == 2:
                rows, hi, lo, first = slice(j0 + t, j0 + t + m), c1_hi, c1_lo, 3
            else:
                rows, hi, lo, first = slice(2 * j0 + t, 2 * (j0 + m - 1) + t + 1, 2), c2_hi, c2_lo, 9
            return first + term, hi[:, rows, cols], lo[:, rows, cols]

        def conv_cols(n):
            return CHUNKS[n][2] * W

        def lo_needed(n):
            layer, j0, m = CHUNKS[n]
            if layer == 2:
                return min(4, (j0 + m - 1) // 8 + 1)
            return 9 if n == 10 else 4 + 3

        @block.tensor
        def _(pe):
            def conv_product(j, k):
                n, term, part = CONV_PRODUCTS[k]
                if term == part == 0:
                    if n == 0:
                        if sure(j):
                            pe.wait_ge(out_done, at(j, N_OUT, 0))
                    elif n >= 2:
                        pe.wait_ge(lo_done, at(j, N_SPLIT, n - 1))
                    if n < 4:
                        pe.wait_ge(xq_lo_done, at(j, 4, n + 1))
                    else:
                        pe.wait_ge(lo_done, at(j, N_SPLIT, lo_needed(n)))
                w, hi, lo = conv_operands(n, term)
                weights = (wc_lo if part == 2 else wc_hi)[:, w * P:(w + 1) * P]
                last = term == TERMS[CHUNKS[n][0]] - 1 and part == 2
                mm = nc.tensor.matmul(conv_ps[n % 2][:, 0:conv_cols(n)], weights, lo if part == 1 else hi,
                                      start=term == part == 0, stop=last)
                if last:
                    mm.then_inc(conv_done, 1)

            def values(i, u):
                if u >= 2 or sure(i):
                    pe.wait_ge(mult_done, at(i, UNITS, u - 1))
                h, tap = u // TAPS, UNIT_TAP[u % TAPS]
                if u < TAPS - 1:
                    pe.wait_ge(pairs_done, at(i, 4, u + 1))
                if u == TAPS - 1:
                    pe.wait_ge(centre_done, at(i, 1, 1))
                for kk in range(K8 // 2):
                    k = h * K8 // 2 + kk
                    src = tap_x[:, tap, 2 * k:2 * k + 2, :].rearrange("p r w -> p (r w)")
                    mm = nc.tensor.matmul(val_ps[u % 2][:, kk * P:(kk + 1) * P], src, val_w_sb[:, :],
                                          start=kk == 0, stop=kk == K8 // 2 - 1, skip_group_check=True)
                mm.then_inc(val_done, 1)

            def transpose_sums(i, n):
                h, g = n // 4, n % 4
                if g == 0:
                    pe.wait_ge(add_done, at(i, 2 * ADDS, ADDS * h + ADDS))
                if n >= 2 or sure(i):
                    pe.wait_ge(agg_sb, at(i, 8, n - 1))
                for kk in range(K8 // 2):
                    at0 = (kk * G + g) * P
                    mm = nc.tensor.transpose(agg_ps[n % 2][:, kk * P:(kk + 1) * P],
                                             prod[:, PROD_BUF[TAPS * h], at0:at0 + P], ident_sb[:, :])
                mm.then_inc(agg_t, 1)

            def pointwise(i, n):
                if n == 0 and sure(i):
                    pe.wait_ge(gn2_v, at(i, GN_V, 0))
                if n % 4 == 0 and (n or sure(i)):
                    pe.wait_ge(x2_part, at(i, 4, n // 2))
                pe.wait_ge(agg_sb, at(i, 8, n + 2))
                for m in (n, n + 1):
                    g = m % 4
                    mm = nc.tensor.matmul(pw_ps[C * g:C * g + C, :], pw_t_sb[:, :], agg[:, m % 2, :],
                                          start=True, stop=True)
                mm.then_inc(pw_pair, 1)

            def gn_sum(sem_v, value, sel, src, dst, done):
                pe.wait_ge(sem_v, value)
                nc.tensor.matmul(dst, sel[:, :], src, start=True, stop=True).then_inc(done, 1)

            def geometry(i):
                pe.wait_ge(xn_done, at(i, 2, 1))
                for k in range(K8):
                    mm = nc.tensor.matmul(geo_ps[:, k * GEO:(k + 1) * GEO],
                                          xc[:, 2 * k:2 * k + 2, :].rearrange("p r w -> p (r w)"),
                                          geo_w_sb[:, :],
                                          start=k == 0, stop=k == K8 - 1, skip_group_check=True)
                mm.then_inc(geo_done, 1)

            def gn1_sums(i, n):
                if n == 0:
                    if sure(i):
                        pe.wait_ge(ch_v, at(i - 1, CH_V, 1))
                    gn_sum(gn1_v, at(i, GN_V, 3), sel1_sb, mv1[:, 0:1], geo_ps[:, 0:1], gn1_pe)
                else:
                    gn_sum(gn1_v, at(i, GN_V, 6), sel1_sb, gn1[:, 2:3], geo_ps[:, 1:2], gn1_pe)

            def gn2_sums(i, n):
                if n == 0:
                    pe.wait_ge(x2_part, at(i, 4, 4))
                    gn_sum(gn2_v, at(i, GN_V, 3), sel1_sb, mv2[:, 0:1], pw_ps[:, 0:1], gn2_pe)
                else:
                    gn_sum(gn2_v, at(i, GN_V, 6), sel1_sb, gn2[:, 2:3], pw_ps[:, 1:2], gn2_pe)

            def convs(i, first, last):
                for k in range(first, last):
                    late = k < len(CONV_PRODUCTS)
                    on(i - 2 if late else i - 1, conv_product, k if late else k - len(CONV_PRODUCTS))

            def body(i):
                on(i - 1, transpose_sums, 2)
                convs(i, 16, 27)
                on(i - 1, pointwise, 0)
                on(i - 1, values, 9)
                on(i - 1, transpose_sums, 3)
                convs(i, 27, 43)
                on(i, values, 0)
                on(i - 1, pointwise, 2)
                convs(i, 43, 101)
                on(i - 1, transpose_sums, 4)
                on(i - 1, transpose_sums, 5)
                convs(i, 101, 106)
                ahead(i + 1, gn1_sums, 0)
                on(i - 1, transpose_sums, 6)
                on(i, values, 1)
                on(i - 1, pointwise, 4)
                on(i - 1, transpose_sums, 7)
                convs(i, 106, 112)
                ahead(i + 1, gn1_sums, 1)
                on(i - 1, pointwise, 6)
                on(i, values, 2)
                convs(i, 112, 130)
                on(i - 1, gn2_sums, 0)
                convs(i, 130, 131)
                on(i, values, 3)
                convs(i, 131, 134)
                on(i, values, 4)
                ahead(i + 1, geometry)
                on(i - 1, gn2_sums, 1)
                convs(i, 134, 180)
                on(i, values, 5)
                on(i, values, 6)
                convs(i, 180, 196)
                on(i, values, 7)
                on(i, transpose_sums, 0)
                on(i, transpose_sums, 1)
                on(i, values, 8)

            pe.wait_ge(front_consts_in, 16 * N_FRONT_CONSTS)
            gn1_sums(0, 0)
            gn1_sums(0, 1)
            geometry(0)
            pe.wait_ge(back_consts_in, 16 * N_BACK_CONSTS)
            pe.wait_ge(pads, N_PADS)
            pe.wait_ge(edges, N_EDGES)
            pe.wait_ge(w_low, 1)
            run_images(pe, body)

        @block.vector
        def _(dve):
            v = nc.vector

            def lo_region(n):
                layer, j0, m = CHUNKS[n]
                ps = conv_ps[n % 2][:, 0:conv_cols(n)].rearrange("p (j w) -> p j w", w=W)
                if layer == 1:
                    sl = slice(1 + j0, 1 + j0 + m)
                    return [(ps, c1_hi[:, sl, 1:1 + W], c1_lo[:, sl, 1:1 + W])]
                half = [(0, P, 0, m)]
                if j0 == 0:
                    half = [(MID, P, 0, 1), (0, P, 1, m)]
                if j0 + m == H // 2 + 1:
                    half = [(0, MID, m - 1, m), (0, P, 0, m - 1)]
                return [(ps[a:b, s:e], c2_hi[a:b, j0 + s:j0 + e, 1:1 + W], c2_lo[a:b, j0 + s:j0 + e, 1:1 + W])
                        for a, b, s, e in half]

            def low_part(j, n):
                dve.wait_ge(hi_done, at(j, N_SPLIT, n + 1))
                for ps, hi, lo in lo_region(n):
                    op = v.tensor_tensor(lo, ps, hi.bitcast(F32), ALU.subtract)
                op.then_inc(lo_done, 1)

            def result(j, n):
                dve.wait_ge(conv_done, at(j, len(CHUNKS), N_SPLIT + n + 1))
                if n == 0:
                    dve.wait_ge(x2r_in, at(j, 256, 256))
                ps = conv_ps[(N_SPLIT + n) % 2][:, :].rearrange("p (j w) -> p j w", w=W)
                v.tensor_tensor(x2r[:, 8 * n:8 * n + 8, :], ps, x2r[:, 8 * n:8 * n + 8, :],
                                ALU.add).then_inc(out_done, 1)

            def mult(i, u):
                h, tap = u // TAPS, UNIT_TAP[u % TAPS]
                dve.wait_ge(val_done, at(i, UNITS, u + 1))
                if u == 0:
                    dve.wait_ge(ch_v, at(i, CH_V, 29))
                s, per, back, n = ((agg_t, 8, 1, 4), (add_done, 8, 1, 5), (add_done, 8, 1, 3), (add_done, 8, 1, 6),
                                   (add_done, 8, 1, 8), (agg_t, 8, 1, 8), (add_done, 8, 0, 1), (add_done, 8, 1, 7),
                                   (add_done, 8, 0, 2), (add_done, 8, 0, 4))[u]
                if not back or sure(i):
                    dve.wait_ge(s, at(i - back, per, n))
                B = K8 // 2 * G
                val = val_ps[u % 2][:, :].rearrange("p (b c) -> p b c", c=C)
                wgt = tapw[:, tap, h * B * R:(h + 1) * B * R].rearrange("p (b r) -> p b r", r=R)
                dst = prod[:, PROD_BUF[u], :].rearrange("p (b r c) -> p b r c", r=R, c=C)
                v.tensor_tensor(dst, val.unsqueeze(2).to_broadcast([P, B, R, C]),
                                wgt.unsqueeze(3).to_broadcast([P, B, R, C]), ALU.mult).then_inc(mult_done, 1)

            def first_sum(i, n):
                if not isinstance(i, int) or i:
                    return
                dve.wait_ge(mult_done, sum_units(n)[1] + 1)
                if n % 4 >= 2:
                    dve.wait_ge(add_done, n)
                a, b = sum_operands(n)
                v.tensor_tensor(a, a, b, ALU.add).then_inc(dve_sum, 1)

            def residual(i, h):
                dve.wait_ge(pw_pair, at(i, 4, 2 * h + 2))
                if h == 0:
                    dve.wait_ge(x_kept, at(i, 64, 64))
                    if sure(i):
                        for g in range(G):
                            dve.wait_ge(x2q_in[g], at(i, 64, 0))
                        dve.wait_ge(x2s_done, at(i, 1, 0))
                def rows(t, parity):
                    return t.rearrange("p (k t w) -> p t k w", t=2, w=W)[:, parity]
                kept = xkeep[:, h * BANK:(h + 1) * BANK]
                half = x2[:, :, 4 * h:4 * h + 4, :]
                for parity in range(2):
                    op = v.scalar_tensor_tensor(half[:, parity], rows(pw_ps[:, :], parity), pw_b_sb[:, 0:1],
                                                rows(kept, parity), ALU.add, ALU.add)
                    op.then_inc(x2_part, 1)
                dve.wait_ge(x2_part, at(i, 4, 2 * h + 2))
                v.bn_stats(st2[:, h, :], half).then_inc(gn2_v, 1)

            def aggregate(i, norm):
                dve.wait_ge(norm.v, at(i, GN_V, 2))
                dve.nop(nofuse=True)
                v.bn_aggr(norm.mv[:, :], norm.st[:, :, :].rearrange("p a b -> p (a b)")).then_inc(norm.v, 1)

            def gn_spread(i, norm):
                t, mv, ps = norm.t, norm.mv, norm.ps
                dve.wait_ge(norm.pe, at(i, 2, 1))
                v.tensor_copy(t[:, 0:1], ps[:, 0:1]).then_inc(norm.v, 1)
                v.tensor_tensor(t[:, 1:2], mv[:, 0:1], ps[:, 0:1], ALU.subtract).then_inc(norm.v, 1)
                dve.wait_ge(norm.v, at(i, GN_V, 5))
                v.scalar_tensor_tensor(t[:, 2:3], t[:, 1:2], t[:, 1:2], mv[:, 1:2],
                                       ALU.mult, ALU.add).then_inc(norm.v, 1)

            def gn_eps(i, norm):
                dve.wait_ge(norm.pe, at(i, 2, 2))
                v.tensor_scalar(norm.t[:, 3:4], norm.ps[:, 1:2], EPS_GN, None, ALU.add).then_inc(norm.v, 1)

            def gn_scale(i, norm):
                t = norm.t
                dve.wait_ge(norm.pow, at(i, 1, 1))
                v.tensor_scalar(t[:, 6:9], masks_sb[:, :], t[:, 4:5], None, ALU.mult).then_inc(norm.v, 1)
                dve.wait_ge(norm.v, at(i, GN_V, 8))
                v.tensor_scalar(t[:, 9:12], t[:, 6:9], t[:, 0:1], -1.0, ALU.mult, ALU.mult).then_inc(norm.v, 1)

            def gn1_stats(i):
                dve.wait_ge(x_in, at(i, 64, 64))
                for n in range(2):
                    v.bn_stats(st1[:, n, :], xraw[:, 1 + 8 * n:9 + 8 * n, :].rearrange("p r w -> p (r w)"))\
                        .then_inc(gn1_v, 1)
                aggregate(i, NORM1)

            def link(i, s, per, k, op):
                op.then_inc(s, 1)
                dve.wait_ge(s, at(i, per, k))

            def tap_weights(i, part):
                gate, theta = geo[:, 0, :], geo[:, 1, :]
                raw = geo[:, 2:4, :]
                e, gs = ch[:, 0, :], ch[:, 1, :]
                th, kk, th2 = ch[:, 2, :], ch[:, 3, :], ch[:, 4, :]
                lb = geo[:, 2, :]
                kern = trig[:, :, :]
                t, w = ch[:, 6:8, :], ch[:, 8:10, :]
                l, spl = ch[:, 10:12, :], ch[:, 12:14, :]

                def step(k, op):
                    link(i, ch_v, CH_V, k, op)

                def need_act(k):
                    dve.wait_ge(ch_a, at(i, CH_A, k))

                if part == 0:
                    dve.wait_ge(geo_done, at(i, 1, 1))
                    src = geo_ps[:, :].rearrange("p (k q j) -> p q k j", q=4, j=G * R)
                    bias = geo_bias_sb[:, :].rearrange("p (q j) -> p q j", q=4).unsqueeze(2)\
                        .to_broadcast([P, 4, K8, G * R])
                    dst = geo[:, :, :].rearrange("p q (k j) -> p q k j", j=G * R)
                    step(1, v.tensor_tensor(dst, src, bias, ALU.add))
                    step(2, v.tensor_scalar(kk, theta, INV_2PI, ROUND, ALU.mult, ALU.add))
                    step(3, v.tensor_scalar(kk, kk, -ROUND, None, ALU.add))
                    step(4, v.scalar_tensor_tensor(th, kk, -TWO_PI_HI, theta, ALU.mult, ALU.add))
                    step(5, v.scalar_tensor_tensor(th, kk, -TWO_PI_LO, th, ALU.mult, ALU.add))
                    step(6, v.tensor_scalar(th2, th, PI_BELOW, -PI_BELOW, ALU.min, ALU.max))
                    g4 = gate.rearrange("p (b r) -> p b r", r=R)
                    step(7, v.tensor_reduce(small[:, 0, :], g4, AX.X, ALU.max))
                    step(8, v.tensor_tensor(gs.rearrange("p (b r) -> p b r", r=R), g4,
                                            small[:, 0, :].unsqueeze(2).to_broadcast([P, K8 * G, R]), ALU.subtract))
                    need_act(2)
                    step(9, v.tensor_scalar(w, t, 1.0, None, ALU.add))
                    step(10, v.scalar_tensor_tensor(t, w, -1.0, t, ALU.add, ALU.subtract))
                if part == 1:
                    need_act(4)
                    step(11, v.tensor_tensor(l, l, t, ALU.subtract))
                    step(12, v.scalar_tensor_tensor(spl, raw, 0.0, l, ALU.max, ALU.add))
                if part == 2:
                    need_act(5)
                    step(13, v.tensor_tensor(w[:, 0, :], spl[:, 1, :], lb, ALU.add))
                    step(14, v.tensor_tensor(w[:, 1, :], spl[:, 1, :], lb, ALU.subtract))
                if part == 3:
                    need_act(10)
                    step(15, v.tensor_tensor(trig[:, 2, :], trig[:, 0, :], trig[:, 1, :], ALU.add))
                    step(16, v.tensor_tensor(trig[:, 3, :], trig[:, 0, :], trig[:, 1, :], ALU.subtract))
                if part == 4:
                    need_act(11)
                    sq = trig2[:, :, :]
                    along, across = (t[:, k, :].unsqueeze(1).to_broadcast([P, 4, NW]) for k in range(2))
                    step(17, v.tensor_tensor(expo[:, :], sq, along, ALU.mult))
                    step(18, v.tensor_tensor(sq, sq, across, ALU.mult))
                    ea = expo[:, :].rearrange("p (h w) n -> p h w n", w=2)
                    eb = sq.rearrange("p (h w) n -> p h w n", w=2)
                    step(19, v.tensor_tensor(ea[:, :, 0], ea[:, :, 0], eb[:, :, 1], ALU.add))
                    step(20, v.tensor_tensor(ea[:, :, 1], ea[:, :, 1], eb[:, :, 0], ALU.add))
                if part == 5:
                    need_act(12)
                    step(21, v.tensor_reduce(kk, kern.rearrange("p t n -> p n t"), AX.X, ALU.add))
                    step(22, v.tensor_scalar(kk, kk, 2.0, 1.0, ALU.mult, ALU.add))
                    step(23, v.tensor_tensor(kk, kk, e, ALU.mult))
                    step(24, v.tensor_reduce(small[:, 1, :], kk.rearrange("p (b r) -> p b r", r=R), AX.X, ALU.add))
                    step(25, v.tensor_reduce(small[:, 2, :], e.rearrange("p (b r) -> p b r", r=R), AX.X, ALU.add))
                    step(26, v.scalar_tensor_tensor(small[:, 3, :], small[:, 2, :], EPS_Z, small[:, 1, :],
                                                    ALU.mult, ALU.add))
                    step(27, v.reciprocal(small[:, 4, :], small[:, 3, :]))
                if part == 6:
                    if sure(i):
                        dve.wait_ge(mult_done, at(i - 1, UNITS, UNITS))
                    step(28, v.tensor_tensor(tapw[:, 0, :].rearrange("p (b r) -> p b r", r=R),
                                             e.rearrange("p (b r) -> p b r", r=R),
                                             small[:, 4, :].unsqueeze(2).to_broadcast([P, K8 * G, R]), ALU.mult))
                    step(29, v.tensor_tensor(tapw[:, 1:TAPS, :], kern,
                                             tapw[:, 0, :].unsqueeze(1).to_broadcast([P, 4, NW]), ALU.mult))

            def split_low(i, n):
                dve.wait_ge(xq_act, at(i, 8, 2 * n + 2))
                rows = slice(8 * n, 8 * n + 8)
                v.tensor_tensor(xq_lo[:, rows, 1:1 + W], x2q[:, 8 * n + 1:8 * n + 9, :],
                                xq_hi[:, rows, 1:1 + W].bitcast(F32), ALU.subtract).then_inc(xq_lo_done, 1)

            def body(i):
                on(i - 1, first_sum, 7)
                ahead(i + 1, gn1_stats)
                on(i - 2, low_part, 4)
                ahead(i, tap_weights, 5)
                on(i - 2, low_part, 5)
                ahead(i, tap_weights, 6)
                on(i - 1, residual, 0)
                on(i - 2, low_part, 6)
                on(i, mult, 0)
                ahead(i + 1, gn_spread, NORM1)
                on(i, mult, 1)
                on(i - 1, residual, 1)
                ahead(i + 1, gn_eps, NORM1)
                on(i - 2, low_part, 7)
                on(i - 1, aggregate, NORM2)
                on(i, mult, 2)
                ahead(i + 1, gn_scale, NORM1)
                on(i - 1, gn_spread, NORM2)
                on(i, mult, 3)
                on(i - 1, gn_eps, NORM2)
                on(i, first_sum, 1)
                on(i - 2, low_part, 8)
                ahead(i + 1, tap_weights, 0)
                on(i - 1, gn_scale, NORM2)
                on(i, mult, 4)
                on(i - 1, split_low, 0)
                ahead(i + 1, tap_weights, 1)
                on(i - 1, split_low, 1)
                on(i - 2, result, 0)
                on(i - 2, result, 1)
                ahead(i + 1, tap_weights, 2)
                on(i - 1, split_low, 2)
                on(i, mult, 5)
                on(i, mult, 6)
                on(i - 1, low_part, 0)
                on(i, mult, 7)
                on(i - 1, split_low, 3)
                on(i - 1, low_part, 1)
                on(i, mult, 8)
                on(i - 1, low_part, 2)
                on(i, first_sum, 5)
                ahead(i + 1, tap_weights, 3)
                on(i, mult, 9)
                on(i - 1, low_part, 3)
                ahead(i + 1, tap_weights, 4)

            for rows in (xraw[0:C, 0, :], xraw[3 * C:P, QR + 1, :], x2q[0:C, 1, :], x2q[3 * C:P, H // 2, :]):
                v.memset(rows, 0.0).then_inc(edges, 1)
            for tile in (c2_hi, c2_lo):
                v.memset(tile[0:MID, 0, 1:1 + W].bitcast(F32), 0.0).then_inc(edges, 1)
                v.memset(tile[MID:P, H // 2, 1:1 + W].bitcast(F32), 0.0).then_inc(edges, 1)
            gn1_stats(0)
            dve.wait_ge(front_consts_in, 16 * N_FRONT_CONSTS)
            gn_spread(0, NORM1)
            gn_eps(0, NORM1)
            gn_scale(0, NORM1)
            for n in range(7):
                if n == 3:
                    dve.wait_ge(w_high, 1)
                    v.tensor_tensor(wc_lo[:, :], w_stage, wc_hi[:, :].bitcast(F32), ALU.subtract).then_inc(w_low, 1)
                tap_weights(0, n)
            dve.wait_ge(back_consts_in, 16 * N_BACK_CONSTS)
            dve.wait_ge(w_low, 1)
            run_images(dve, body)

        @block.scalar
        def _(act):
            s = nc.scalar
            C_PI2, C_EPSB, C_MH, C_PH = (consts_sb[:, k:k + 1] for k in range(4))

            def hi_part(j, n):
                act.wait_ge(conv_done, at(j, len(CHUNKS), n + 1))
                layer, j0, m = CHUNKS[n]
                ps = conv_ps[n % 2][:, 0:conv_cols(n)].rearrange("p (j w) -> p j w", w=W)
                if layer == 1:
                    parts = [(ps, c1_hi[:, 1 + j0:1 + j0 + m, 1:1 + W])]
                else:
                    half = [(0, P, 0, m)]
                    if j0 == 0:
                        half = [(MID, P, 0, 1), (0, P, 1, m)]
                    if j0 + m == H // 2 + 1:
                        half = [(0, MID, m - 1, m), (0, P, 0, m - 1)]
                    parts = [(ps[a:b, q:r], c2_hi[a:b, j0 + q:j0 + r, 1:1 + W]) for a, b, q, r in half]
                for src, dst in parts:
                    op = s.activation(dst, src, ACT.Copy)
                op.then_inc(hi_done, 1)

            def sums_out(i, n):
                act.wait_ge(agg_t, at(i, 8, n + 1))
                if n >= 2 or sure(i):
                    act.wait_ge(pw_pair, at(i, 4, n // 2))
                s.activation(agg[:, n % 2, :], agg_ps[n % 2][:, :], ACT.Copy).then_inc(agg_sb, 1)

            def norm1(i):
                act.wait_ge(gn1_v, at(i, GN_V, GN_V))
                if sure(i):
                    act.wait_ge(geo_done, at(i, 1, 0))
                    act.wait_ge(centre_done, at(i, 1, 0))
                    act.wait_ge(pairs_done, at(i, 4, 0))
                s.activation(xc[:, :, :], xraw[:, 1:QR + 1, :], ACT.Identity,
                             scale=gn1[:, 6:7], bias=gn1[:, 9:10]).then_inc(xn_done, 1)
                for row, n, m in ((0, 1, 1), (QR + 1, 1, 2), (1, QR, 0)):
                    op = s.activation(xn[:, row:row + n, 1:1 + W], xraw[:, row:row + n, :], ACT.Identity,
                                      scale=gn1[:, 6 + m:7 + m], bias=gn1[:, 9 + m:10 + m])
                op.then_inc(xn_done, 1)

            def centre(i):
                if sure(i):
                    act.wait_ge(val_done, at(i, UNITS, 0))
                act.wait_ge(xn_done, at(i, 2, 1))
                s.activation(tap_x[:, 0], xc[:, :, :], ACT.Copy).then_inc(centre_done, 1)

            def tap_weights(i, part):
                gs = ch[:, 1, :]
                th2, tha = ch[:, 4, :], ch[:, 5, :]
                t, w, l, spl = ch[:, 6:8, :], ch[:, 8:10, :], ch[:, 10:12, :], ch[:, 12:14, :]
                lb = geo[:, 2, :]

                def need(k):
                    act.wait_ge(ch_v, at(i, CH_V, k))

                def step(k, op):
                    op.then_inc(ch_a, 1)
                    act.wait_ge(ch_a, at(i, CH_A, k))

                if part == 0:
                    need(1)
                    step(1, s.activation(t, geo[:, 2:4, :], ACT.Abs))
                    step(2, s.activation(t, t, ACT.Exp, scale=-1.0))
                    need(8)
                    step(3, s.activation(ch[:, 0, :], gs, ACT.Exp))
                    need(10)
                    step(4, s.activation(l, w, ACT.Ln))
                if part == 1:
                    need(12)
                    step(5, s.activation(lb, spl[:, 0, :], ACT.Ln, bias=C_EPSB))
                    need(14)
                    step(6, s.activation(t[:, 0, :], w[:, 0, :], ACT.Exp, scale=-2.0, bias=C_MH))
                    step(7, s.activation(t[:, 1, :], w[:, 1, :], ACT.Exp, scale=2.0, bias=C_PH))
                    step(8, s.activation(tha, th2, ACT.Abs))
                    step(9, s.activation(trig[:, 1, :], th2, ACT.Sin))
                    step(10, s.activation(trig[:, 0, :], tha, ACT.Sin, scale=-1.0, bias=C_PI2))
                    act.nop(nofuse=True)
                    s.preload_act_table_set(EXP_SET)
                if part == 2:
                    need(16)
                    step(11, s.activation(trig2[:, :, :], trig[:, :, :], ACT.Square))
                    need(20)
                    step(12, s.activation(trig[:, :, :], expo[:, :], ACT.Exp, scale=-1.0))

            def split_high(i, n):
                if n == 0:
                    act.wait_ge(gn2_v, at(i, GN_V, GN_V))
                    if sure(i):
                        act.wait_ge(conv_done, at(i - 1, len(CHUNKS), 4))
                for g in ((0, 1), (2,), (3,), ())[n]:
                    act.wait_ge(x2q_in[g], at(i, 64, 64))
                parts = [(8 * n, 8 * n + 8, 0)]
                if n == 0:
                    parts = [(0, 1, 1), (1, 8, 0)]
                if n == 3:
                    parts = [(H // 2 - 1, H // 2, 2), (24, H // 2 - 1, 0)]
                for a, b, m in parts:
                    op = s.activation(x2q[:, a + 1:b + 1, :], x2q[:, a + 1:b + 1, :], ACT.Identity,
                                      scale=gn2[:, 6 + m:7 + m], bias=gn2[:, 9 + m:10 + m])
                op.then_inc(xq_act, 1)
                act.wait_ge(xq_act, at(i, 8, 2 * n + 1))
                s.activation(xq_hi[:, 8 * n:8 * n + 8, 1:1 + W], x2q[:, 8 * n + 1:8 * n + 9, :],
                             ACT.Copy).then_inc(xq_act, 1)

            def quad_rows(i):
                act.wait_ge(x2_part, at(i, 4, 4))
                if sure(i):
                    act.wait_ge(x2r_in, at(i, 256, 0))
                for parity in range(2):
                    dst = x2s[:, parity::2, :, :]
                    src = x2[:, parity, :, :].rearrange("p (q a) w -> p a q w", a=2)
                    op = s.activation(dst, src, ACT.Copy)
                op.then_inc(x2s_done, 1)

            def body(i):
                on(i - 2, hi_part, 6)
                on(i - 1, sums_out, 4)
                on(i - 1, sums_out, 5)
                ahead(i, centre)
                on(i - 1, sums_out, 6)
                on(i - 1, sums_out, 7)
                on(i - 2, hi_part, 7)
                on(i - 2, hi_part, 8)
                ahead(i + 1, norm1)
                ahead(i + 1, tap_weights, 0)
                on(i - 1, split_high, 0)
                on(i - 1, split_high, 1)
                on(i - 1, split_high, 2)
                ahead(i + 1, tap_weights, 1)
                on(i - 1, hi_part, 0)
                on(i, sums_out, 0)
                on(i - 1, split_high, 3)
                on(i, sums_out, 1)
                on(i - 1, hi_part, 1)
                on(i - 1, quad_rows)
                on(i, sums_out, 2)
                on(i - 1, hi_part, 2)
                on(i, sums_out, 3)
                on(i - 1, hi_part, 3)
                ahead(i + 1, tap_weights, 2)
                on(i - 1, hi_part, 4)
                on(i - 1, hi_part, 5)

            s.preload_act_table_set(EXP_SET)
            act.wait_ge(front_consts_in, 16 * N_FRONT_CONSTS)
            act.wait_ge(edges, N_EDGES)
            norm1(0)
            centre(0)
            act.wait_ge(weights_in, 16 * 3)
            s.activation(wc_hi[:, :], w_stage, ACT.Copy).then_inc(w_high, 1)
            for n in range(3):
                tap_weights(0, n)
            run_images(act, body)

        @block.gpsimd
        def _(pool):
            p = nc.gpsimd

            def rstd(i, norm):
                t = norm.t
                pool.wait_ge(norm.v, at(i, GN_V, 7))
                p.tensor_tensor(t[:, 4:5], t[:, 3:4], t[:, 5:6], ALU.pow).then_inc(norm.pow, 1)

            def add_products(i, n):
                if isinstance(i, int) and i == 0 and n in DVE_SUMS:
                    pool.wait_ge(add_done, n)
                    pool.wait_ge(dve_sum, DVE_SUMS.index(n) + 1)
                    pool.nop(nofuse=True).then_inc(add_done, 1)
                    return
                pool.wait_ge(mult_done, at(i, UNITS, sum_units(n)[1] + 1))
                if n % 4 >= 2:
                    pool.wait_ge(add_done, at(i, 2 * ADDS, n))
                a, b = sum_operands(n)
                p.tensor_tensor(a, a, b, ALU.add).then_inc(add_done, 1)

            def shifted_sum(i, n):
                up, mid, down = slice(0, QR), slice(1, QR + 1), slice(2, QR + 2)
                left, here, right = slice(0, W), slice(1, 1 + W), slice(2, 2 + W)
                a, b = (((mid, left), (mid, right)), ((up, here), (down, here)),
                        ((up, left), (down, right)), ((up, right), (down, left)))[n]
                if n == 0:
                    pool.wait_ge(xn_done, at(i, 2, 2))
                if sure(i):
                    pool.wait_ge(val_done, at(i - 1, UNITS, TAPS + 1 + n))
                p.tensor_tensor(tap_x[:, 1 + n], xn[:, a[0], a[1]], xn[:, b[0], b[1]],
                                ALU.add).then_inc(pairs_done, 1)

            def body(i):
                ahead(i, shifted_sum, 2)
                ahead(i, shifted_sum, 3)
                ahead(i + 1, rstd, NORM1)
                on(i, add_products, 0)
                on(i - 1, rstd, NORM2)
                on(i, add_products, 1)
                on(i, add_products, 2)
                on(i, add_products, 3)
                ahead(i + 1, shifted_sum, 0)
                on(i, add_products, 4)
                on(i, add_products, 5)
                on(i, add_products, 6)
                on(i, add_products, 7)
                ahead(i + 1, shifted_sum, 1)

            for tile in (xn, xq_hi, xq_lo, c1_hi, c1_lo, c2_hi, c2_lo):
                for col in (0, PW - 1):
                    p.memset(tile[:, :, col:col + 1].bitcast(F32), 0.0).then_inc(pads, 1)
            for tile in (c1_hi, c1_lo):
                for row in (0, H // 2 + 1):
                    p.memset(tile[:, row, 1:1 + W].bitcast(F32), 0.0).then_inc(pads, 1)
            p.memset(gn1[:, 5:6], -0.5).then_inc(pads, 1)
            p.memset(gn2[:, 5:6], -0.5).then_inc(pads, 1)
            pool.wait_ge(pads, N_PADS)
            rstd(0, NORM1)
            for n in range(4):
                shifted_sum(0, n)
            run_images(pool, body)


def kernel(**inputs):
    import numpy as np
    import concourse.bacc as bacc
    from concourse import mybir as mb
    from concourse.bass_utils import run_bass_kernel_spmd

    a = {k: np.asarray(v) for k, v in inputs.items()}
    f = np.float32
    rows = np.concatenate([a["L0_conv_gate_w"], a["L0_conv_geom_w"]], axis=0).reshape(4, R, C)
    bias = np.concatenate([a["L0_conv_gate_b"], a["L0_conv_geom_b"]], axis=0).reshape(4, R)
    geo_w = np.zeros((G, C, 4, G, R), f)
    geo_bias = np.zeros((P, 4, G, R), f)
    val_w = np.zeros((G, C, G, C), f)
    for g in range(G):
        geo_w[g, :, :, g, :] = rows.transpose(2, 0, 1)
        geo_bias[:, :, g, :] = bias
        val_w[g, :, g, :] = a["L0_conv_value_w"].T
    pw_b = np.zeros((G, C, 1), f)
    pw_b[:, :, 0] = a["L0_conv_pw_b"]

    def banded(w, rows_in, rows_out, groups, step):
        o, c = w.shape[:2]
        m = np.zeros((rows_in, c, groups, 3, rows_out, o), f)
        for t in range(groups):
            for ri in range(rows_in):
                for ro in range(rows_out):
                    ky = step * t + ri - ro
                    if 0 <= ky <= 2:
                        m[ri, :, t, :, ro, :] = w[:, :, ky, :].transpose(1, 2, 0)
        return m.reshape(rows_in * c, groups * 3 * rows_out * o)

    sel_quarter = np.zeros((G, C, G, C), f)
    for c in range(C):
        sel_quarter[:, c, :, c] = 1.0 / G
    masks = np.ones((P, 3), f)
    masks[0:C, 1] = 0.0
    masks[P - C:P, 2] = 0.0
    consts = np.zeros((P, 4), f)
    consts[:, :] = np.array([1.5707963267948966, EPS_BASE, -2 * MIN_HYP, 2 * MIN_HYP], f)
    arrays = {
        "x": np.ascontiguousarray(a["x"]), "geo_w": geo_w.reshape(P, GEO), "geo_bias": geo_bias.reshape(P, GEO),
        "val_w": val_w.reshape(P, P), "pw_t": np.ascontiguousarray(a["L0_conv_pw_w"].T), "pw_b": pw_b.reshape(P, 1),
        "w1": banded(a["L1_conv_w1"], 4, 2, 1, 0), "w2": banded(a["L1_conv_w2"], 2, 2, 2, 2),
        "w3": banded(a["L1_conv_w3"], 2, 4, 3, 2), "ident": np.eye(P, dtype=f),
        "sel_quarter": sel_quarter.reshape(P, P),
        "masks": masks, "consts": consts,
    }
    nc = bacc.Bacc("TRN2", target_bir_lowering=False, num_devices=1)
    args = [nc.dram_tensor(f"in_{k}", v.shape, mb.dt.from_np(v.dtype), kind="ExternalInput").ap()
            for k, v in arrays.items()]
    out = nc.dram_tensor("out_y", (IMAGES, C, H, W), F32, kind="ExternalOutput").ap()
    conv_l0_l1_kernel(nc, *args, out)
    r = run_bass_kernel_spmd(nc, [{f"in_{k}": v for k, v in arrays.items()}], core_ids=[0])
    return r.results[0]["out_y"]
```
